# Optimizing a Trainium2 kernel written in Bass

```python
import numpy as np
import jax
import jax.numpy as jnp

def _softmax(x, axis=-1):
    return jax.nn.softmax(x, axis=axis)
def _gelu(x):
    return jax.nn.gelu(x, approximate=True)
def _silu(x):
    return jax.nn.silu(x)
def _sigmoid(x):
    return jax.nn.sigmoid(x)
def _layernorm(x, axis=-1, eps=1e-5):
    m = jnp.mean(x, axis=axis, keepdims=True)
    v = jnp.var(x, axis=axis, keepdims=True)
    return (x - m) / jnp.sqrt(v + eps)
def _scatter_add(tgt, idx, src, axis=0):
    return tgt.at[idx].add(src)
def _segment_sum(src, seg, n):
    return jax.ops.segment_sum(src, seg, n)

kernel_name = 'mk_adj_preln_d2_adj_512_1dd73d'

def setup_inputs(seed: int = 0):
    np.random.seed(seed)
    _w = jnp.asarray
    def _rec_inputs():
        import jax
        import jax.numpy as jnp
        _gk = jax.random.key(seed)
        x = -0.0005207 + 1.001 * jax.random.normal(jax.random.fold_in(_gk, 1), (128, 128, 512), jnp.float32)
        _a = jax.random.bernoulli(jax.random.fold_in(_gk, 2), 0.0625, (128, 128, 128))
        _a = jnp.logical_or(_a, jnp.eye(128, dtype=bool))
        _af = _a.astype(jnp.float32)
        adj = _af
        return x, adj
    x, adj = _rec_inputs()
    def _L0_gnn_setup():
        import jax, jax.numpy as jnp
        import numpy as np
        N = 4096
        F_IN = 512
        UNITS = 64
        HEADS = 8
        NEG_BIG = -10000000000.0
        key = jax.random.key(seed)
        ks = jax.random.split(key, 7)
        X = jax.random.normal(ks[0], (1, N, F_IN), dtype=jnp.float32)
        A = (jax.random.uniform(ks[1], (1, N, N)) < 0.008).astype(jnp.float32)
        A = jnp.maximum(A, jnp.eye(N, dtype=jnp.float32)[None])
        glorot = lambda k, shp: jax.random.uniform(k, shp, jnp.float32, -1.0, 1.0) * jnp.sqrt(6.0 / (shp[-2] + shp[-1]))
        W = glorot(ks[2], (HEADS, F_IN, UNITS))
        b = jnp.zeros((HEADS, UNITS), dtype=jnp.float32)
        a_self = glorot(ks[3], (HEADS, UNITS, 1))[..., 0]
        a_neigh = glorot(ks[4], (HEADS, UNITS, 1))[..., 0]
        return {'X': X, 'A': A, 'W': W, 'b': b, 'a_self': a_self, 'a_neigh': a_neigh}
    _L0_gnn_all = _L0_gnn_setup()
    _L0_gnn_in = {k: v for k, v in _L0_gnn_all.items() if k in ('W', 'b', 'a_self', 'a_neigh', )}
    del _L0_gnn_all

    def _L1_gnn_setup():
        import jax, jax.numpy as jnp
        import numpy as np
        EPS_LN = 1e-05

        def hypergraph_conv(x, adj, W, b):
            N, C, _ = adj.shape
            H = (adj != 0).astype(x.dtype)
            w = adj.reshape(N, -1)[:, :C]
            xw = jnp.einsum('ncd,hd->nch', x, W)
            Dn = jnp.einsum('nce,ne->nc', H, w)
            Dn = jnp.where(Dn > 0, 1.0 / Dn, 0.0)
            Be = H.sum(axis=1)
            Be = jnp.where(Be > 0, 1.0 / Be, 0.0)
            m = Be[:, :, None] * jnp.einsum('nce,nch->neh', H, xw)
            out = Dn[:, :, None] * jnp.einsum('nce,neh->nch', H, m)
            return out + b

        def layer_norm(x, g, b):
            mu = jnp.mean(x, axis=-1, keepdims=True)
            var = jnp.var(x, axis=-1, keepdims=True)
            return (x - mu) * jax.lax.rsqrt(var + EPS_LN) * g + b
        key = jax.random.key(seed)
        ks = jax.random.split(key, 4)
        N, C, Din, Dh, Dout = (16, 1024, 512, 1024, 512)
        x = jax.random.normal(ks[0], (N, C, Din), dtype=jnp.float32)
        adj = jax.random.uniform(ks[1], (N, C, C), dtype=jnp.float32, minval=0.1, maxval=1.0)
        W1 = jax.random.normal(ks[2], (Dh, Din), dtype=jnp.float32) * (1.0 / np.sqrt(Din))
        b1 = jnp.zeros((Dh,), dtype=jnp.float32)
        gamma = jnp.ones((Dh,), dtype=jnp.float32)
        beta = jnp.zeros((Dh,), dtype=jnp.float32)
        W2 = jax.random.normal(ks[3], (Dout, Dh), dtype=jnp.float32) * (1.0 / np.sqrt(Dh))
        b2 = jnp.zeros((Dout,), dtype=jnp.float32)
        return {'x': x, 'adj': adj, 'W1': W1, 'b1': b1, 'gamma': gamma, 'beta': beta, 'W2': W2, 'b2': b2}
    _L1_gnn_all = _L1_gnn_setup()
    _L1_gnn_in = {k: v for k, v in _L1_gnn_all.items() if k in ('W1', 'b1', 'gamma', 'beta', 'W2', 'b2', )}
    del _L1_gnn_all

    return {
        "x": x,
        "adj": adj,
        "L0_gnn_W": _L0_gnn_in["W"],
        "L0_gnn_b": _L0_gnn_in["b"],
        "L0_gnn_a_self": _L0_gnn_in["a_self"],
        "L0_gnn_a_neigh": _L0_gnn_in["a_neigh"],
        "L1_gnn_W1": _L1_gnn_in["W1"],
        "L1_gnn_b1": _L1_gnn_in["b1"],
        "L1_gnn_gamma": _L1_gnn_in["gamma"],
        "L1_gnn_beta": _L1_gnn_in["beta"],
        "L1_gnn_W2": _L1_gnn_in["W2"],
        "L1_gnn_b2": _L1_gnn_in["b2"],
    }

def reference(x, adj, L0_gnn_W, L0_gnn_b, L0_gnn_a_self, L0_gnn_a_neigh, L1_gnn_W1, L1_gnn_b1, L1_gnn_gamma, L1_gnn_beta, L1_gnn_W2, L1_gnn_b2):
    import jax
    import jax.numpy as jnp
    def _L0_gnn_ref(X, A, W, b, a_self, a_neigh):
        import jax, jax.numpy as jnp
        import numpy as np
        N = 4096
        F_IN = 512
        UNITS = 64
        HEADS = 8
        NEG_BIG = -10000000000.0
        feats = jnp.einsum('bnf,hfu->bhnu', X, W)
        e_self = jnp.einsum('bhnu,hu->bhn', feats, a_self)
        e_neigh = jnp.einsum('bhnu,hu->bhn', feats, a_neigh)
        dense = e_self[..., :, None] + e_neigh[..., None, :]
        dense = jax.nn.leaky_relu(dense, negative_slope=0.2)
        dense = dense + NEG_BIG * (1.0 - A[:, None, :, :])
        att = jax.nn.softmax(dense, axis=-1)
        out = jnp.einsum('bhij,bhju->bhiu', att, feats) + b[None, :, None, :]
        out = out.transpose(0, 2, 1, 3).reshape(X.shape[0], X.shape[1], HEADS * UNITS)
        return jax.nn.relu(out)

    def _L1_gnn_ref(x, adj, W1, b1, gamma, beta, W2, b2):
        import jax, jax.numpy as jnp
        import numpy as np
        EPS_LN = 1e-05

        def hypergraph_conv(x, adj, W, b):
            N, C, _ = adj.shape
            H = (adj != 0).astype(x.dtype)
            w = adj.reshape(N, -1)[:, :C]
            xw = jnp.einsum('ncd,hd->nch', x, W)
            Dn = jnp.einsum('nce,ne->nc', H, w)
            Dn = jnp.where(Dn > 0, 1.0 / Dn, 0.0)
            Be = H.sum(axis=1)
            Be = jnp.where(Be > 0, 1.0 / Be, 0.0)
            m = Be[:, :, None] * jnp.einsum('nce,nch->neh', H, xw)
            out = Dn[:, :, None] * jnp.einsum('nce,neh->nch', H, m)
            return out + b

        def layer_norm(x, g, b):
            mu = jnp.mean(x, axis=-1, keepdims=True)
            var = jnp.var(x, axis=-1, keepdims=True)
            return (x - mu) * jax.lax.rsqrt(var + EPS_LN) * g + b
        h = jax.nn.relu(hypergraph_conv(x, adj, W1, b1))
        h = layer_norm(h, gamma, beta)
        y = hypergraph_conv(h, adj, W2, b2)
        return y + x

    h = jnp.maximum(_layernorm(x, axis=-1), 0.0)
    x = x + _L0_gnn_ref(h, adj, L0_gnn_W, L0_gnn_b, L0_gnn_a_self, L0_gnn_a_neigh)
    h = jnp.maximum(_layernorm(x, axis=-1), 0.0)
    x = x + _L1_gnn_ref(h, adj, L1_gnn_W1, L1_gnn_b1, L1_gnn_gamma, L1_gnn_beta, L1_gnn_W2, L1_gnn_b2)
    return x


_drawn_inputs = setup_inputs


def setup_inputs(seed=0):
    import zlib

    import numpy as np

    out = dict(_drawn_inputs(seed))
    spreads = {'L0_gnn_b': (0.0, 0.1),
     'L1_gnn_b1': (0.0, 0.1),
     'L1_gnn_gamma': (1.0, 0.2),
     'L1_gnn_beta': (0.0, 0.1),
     'L1_gnn_b2': (0.0, 0.359)}
    factors = {'L0_gnn_a_self': 3.605}
    for name, (base, spread) in spreads.items():
        noise = np.random.default_rng([zlib.crc32(name.encode()), seed]).standard_normal(out[name].shape)
        drawn = base * np.exp(spread * noise) if base else spread * noise
        out[name] = jnp.asarray(drawn.astype(out[name].dtype))
    for name, factor in factors.items():
        out[name] = (out[name] * factor).astype(out[name].dtype)
    return out
```

```python
import concourse.bass as bass
from concourse import mybir
from contextlib import ExitStack

F32 = mybir.dt.float32
F32R = mybir.dt.float32r
ALU = mybir.AluOpType
ACT = mybir.ActivationFunctionType
X = mybir.AxisListType.X

P = 128
AHEAD = 3
UNROLL = 4
EPS = 1e-5
SLOPE = 0.2
NEG_BIG = -1e10
TINY = 1e-30


class Graph:

    def __init__(self, base, loop=None):
        self.base, self.loop = base, loop

    def plus(self, n):
        return Graph(self.base + n, self.loop)

    def within(self, total):
        return self.loop is not None or 0 <= self.base < total

    def slot(self, ring):
        return self.base % ring

    def has(self, back):
        return self.loop is not None or self.base >= back

    def count(self, back=0, per=1):
        n = (self.base + 1 - back) * per
        return n if self.loop is None else self.loop * (UNROLL * per) + n

    def uses(self, ring, per):
        n = (self.base // ring + 1) * per
        return n if self.loop is None else self.loop * (UNROLL // ring * per) + n


def turns(eng, turn, total):
    loops = (total - AHEAD - 2) // UNROLL
    for t in range(-AHEAD, 1):
        turn(Graph(t))
    with eng.Fori(0, loops) as k:
        for u in range(1, UNROLL + 1):
            turn(Graph(u, k))
    for t in range(1 + loops * UNROLL, total + 1):
        turn(Graph(t))


def gnn_two_layers(nc, x, adj2, W0T, b0, a_self, a_neigh, W1T, b1, gammaT, betaT, W2T, b2, out):
    NG, N, D = x.shape
    HEADS = a_self.shape[0]
    UN = D // HEADS
    DH = W1T.shape[1]
    DC, HC = D // P, DH // P
    HALF = 512
    HH = HEADS // 2
    CB = HC // 2
    UE = UN + 1
    HN = HEADS * N

    ctx = ExitStack()
    with ctx:
        def sb(name, shape, dt=F32):
            return ctx.enter_context(nc.sbuf_tensor(name, shape, dt))

        def sem(name):
            return ctx.enter_context(nc.semaphore(name))

        W0_hi, W0_lo = (sb(n, [P, DC, D], F32R) for n in ("W0_hi", "W0_lo"))
        Wa_hi, Wa_lo = (sb(n, [P, DC, 64], F32R) for n in ("Wa_hi", "Wa_lo"))
        W1_hi, W1_lo = (sb(n, [P, DC, DH], F32R) for n in ("W1_hi", "W1_lo"))
        W2_hi, W2_lo = (sb(n, [P, HC, D], F32R) for n in ("W2_hi", "W2_lo"))
        stage = sb("stage", [P, 2, 4 * HALF])
        ident = sb("ident", [P, P])
        ident_r = sb("ident_r", [P, P], F32R)
        ones = sb("ones", [P, P])
        halfpow = sb("halfpow", [P, 1])
        eps = sb("eps", [P, 1])
        b0_bc = sb("b0_bc", [P, D])
        b1_bc = sb("b1_bc", [P, DH])
        b2_bc = sb("b2_bc", [P, D])
        t_bc = sb("t_bc", [P, D])
        gamma_sb = sb("gamma_sb", [P, HC])
        beta_sb = sb("beta_sb", [P, HC])
        head_sel = sb("head_sel", [64, HEADS, N])
        lo_rows8 = sb("lo_rows8", [64, HEADS])
        lo_rows = sb("lo_rows", [64, 1])
        x_in = sb("x_in", [P, 4, D])
        adj_in = sb("adj_in", [P, 4, 2, N])
        inc = sb("inc", [P, 2, 2, N])
        mask = sb("mask", [P, N], F32R)
        cnt = sb("cnt", [P, 2])
        inv0 = sb("inv0", [P, 2])
        inv = sb("inv", [P, 4, 2])
        beT = sb("beT", [P, N])
        G = sb("G", [P, 4, N])
        st0 = sb("st0", [P, 6])
        st1 = sb("st1", [P, 6])
        st2 = sb("st2", [P, 2, 6])
        mv0 = sb("mv0", [P, 2])
        mv1 = sb("mv1", [P, 2])
        mv2 = sb("mv2", [P, 2])
        ve0, ve1, ve2 = sb("ve0", [P, 1]), sb("ve1", [P, 1]), sb("ve2", [P, 1])
        rs0, rs1, rs2 = sb("rs0", [P, 1]), sb("rs1", [P, 1]), sb("rs2", [P, 1])
        nb1 = sb("nb1", [P, 1])
        xn = sb("xn", [P, D])
        h0_hi, h0_lo = sb("h0_hi", [P, D], F32R), sb("h0_lo", [P, D], F32R)
        feats = sb("feats", [P, 2, HEADS, UE])
        e_sb = sb("e_sb", [P, 64])
        e_hi = sb("e_hi", [64, N], F32R)
        en_parts = sb("en_parts", [64, N])
        es_lhs = sb("es_lhs", [64, N], F32R)
        en_rhs = sb("en_rhs", [64, HEADS, N], F32R)
        att = sb("att", [P, HEADS, N])
        neg_max = sb("neg_max", [P, HEADS])
        attT = sb("attT", [P, HEADS, N])
        rden = sb("rden", [P, HEADS])
        o_sc = sb("o_sc", [P, D])
        x1 = sb("x1", [P, 2, D])
        h = sb("h", [P, 2, D])
        rest = sb("rest", [P, 2, D])
        hg_hi, hg_lo = sb("hg_hi", [P, D], F32R), sb("hg_lo", [P, D], F32R)
        r = sb("r", [P, DH])
        rT_hi, rT_lo = sb("rT_hi", [P, DH], F32R), sb("rT_lo", [P, DH], F32R)
        z = sb("z", [P, D])
        y = sb("y", [P, 2, D])

        def bank(name, n=1):
            return ctx.enter_context(nc.psum_tensor(name, [P, n * HALF], F32))

        p_w1a = bank("p_w1a")
        p_w1b = bank("p_w1b")
        p_att = bank("p_att", 2)
        p_ta = bank("p_ta")
        p_tb = bank("p_tb")
        p_f = bank("p_f")
        p_s = bank("p_s")
        p_e = p_s[:, 0:64]
        p_eT = p_s[0:64, 64:192]
        p_cnt = p_s[:, 192:194]
        p_G = p_s[:, 256:384]
        p_scores = p_att[:, :]
        p_o = p_att[:, :].rearrange("p (b c) -> p b c", b=2)[:, :, 0:HH * UE].rearrange("p b (h u) -> p b h u", u=UE)

        s_in = [sem(f"s_in{i}") for i in range(4)]
        s_out = [sem(f"s_out{i}") for i in range(2)]
        s_small = sem("s_small")
        s_stage = [sem(f"s_stage{i}") for i in range(2)]
        k_hi, k_lo, k_const, k_ones = sem("k_hi"), sem("k_lo"), sem("k_const"), sem("k_ones")
        k_wa, k_wa_hi, k_wa_lo, k_cols = sem("k_wa"), sem("k_wa_hi"), sem("k_wa_lo"), sem("k_cols")
        k_mean, k_mean_sb, k_cent, k_t, k_lorow = sem("k_mean"), sem("k_mean_sb"), sem("k_cent"), sem("k_t"), sem("k_lorow")
        s_stats0, s_mv0, s_ve0, s_rs0, s_xn, s_xnT = (sem("s_" + n) for n in ("stats0", "mv0", "ve0", "rs0", "xn", "xnT"))
        s_h0_hi, s_h0_lo, s_feats, s_feats_sb, s_e_sb = (sem("s_" + n) for n in ("h0_hi", "h0_lo", "feats", "feats_sb", "e_sb"))
        s_eT, s_e_hi, s_es_lhs, s_en_parts, s_en_rhs = (sem("s_" + n) for n in ("eT", "e_hi", "es_lhs", "en_parts", "en_rhs"))
        s_mask, s_scores, s_sloped, s_leaky, s_max = (sem("s_" + n) for n in ("mask", "scores", "sloped", "leaky", "max"))
        s_exp, s_attT, s_attT_sb, s_o, s_rden, s_osc, s_x1 = (sem("s_" + n) for n in ("exp", "attT", "attT_sb", "o", "rden", "osc", "x1"))
        s_inc, s_cnt, s_cnt1, s_inv0, s_inv, s_beT, s_G, s_G_sb = (sem("s_" + n) for n in ("inc", "cnt", "cnt1", "inv0", "inv", "beT", "G", "G_sb"))
        s_stats1, s_mv1, s_ve1, s_rs1, s_nb1, s_h, s_xh, s_rest = (sem("s_" + n) for n in ("stats1", "mv1", "ve1", "rs1", "nb1", "h", "xh", "rest"))
        s_hg, s_hg_hi, s_hg_lo, s_w1, s_pre, s_r = (sem("s_" + n) for n in ("hg", "hg_hi", "hg_lo", "w1", "pre", "r"))
        s_stats2, s_mv2, s_ve2, s_rs2, s_rT, s_rT_hi, s_rT_lo = (sem("s_" + n) for n in ("stats2", "mv2", "ve2", "rs2", "rT", "rT_hi", "rT_lo"))
        s_w2, s_z, s_y, s_y_sb = (sem("s_" + n) for n in ("w2", "z", "y", "y_sb"))

        block = ctx.enter_context(nc.Block())

        def piece(n):
            return stage[:, n % 2, :].rearrange("p (c n) -> p c n", c=4)

        PIECES = [
            (W0T.rearrange("(c p) n -> p c n", p=P), W0_hi[:, :, :], W0_lo[:, :, :]),
            (W1T.rearrange("(c p) n -> p c n", p=P)[:, :, 0:HALF], W1_hi[:, :, 0:HALF], W1_lo[:, :, 0:HALF]),
            (W1T.rearrange("(c p) n -> p c n", p=P)[:, :, HALF:DH], W1_hi[:, :, HALF:DH], W1_lo[:, :, HALF:DH]),
            (W2T.rearrange("(c p) n -> p c n", p=P)[:, 0:CB, :], W2_hi[:, 0:CB, :], W2_lo[:, 0:CB, :]),
            (W2T.rearrange("(c p) n -> p c n", p=P)[:, CB:HC, :], W2_hi[:, CB:HC, :], W2_lo[:, CB:HC, :]),
        ]
        SMALL = 7
        wa_raw = r[:, 0:DC * 64].rearrange("p (c n) -> p c n", c=DC)
        prod = att[:, :, :].rearrange("p h n -> p (h n)")

        @block.sync
        def _(sp):
            def load(g):
                if g.has(4):
                    sp.wait_ge(s_x1, g.count(4))
                    sp.wait_ge(s_inc, g.count(4))
                    sp.wait_ge(s_mask, g.count(4))
                    sp.wait_ge(s_cnt, g.count(4))
                s = g.slot(4)
                n = g.base if g.loop is None else g.loop * UNROLL + g.base
                sp.dma_start(x_in[:, s, :], x[bass.ds(n, 1), :, :].rearrange("a p d -> p (a d)")).then_inc(s_in[s], 16)
                sp.dma_start(adj_in[:, s, :, :], adj2[bass.ds(n, 1), :, :, :].rearrange("a p t n -> p (a t) n")).then_inc(s_in[s], 16)

            def load_piece(n):
                if n >= 2:
                    sp.wait_ge(k_hi, n - 1)
                    sp.wait_ge(k_lo, n - 1)
                sp.dma_start(piece(n), PIECES[n][0]).then_inc(s_stage[n % 2], 16)

            def bc(v, n):
                return v.rearrange("(a n) -> a n", a=1).broadcast_to([P, n])

            load(Graph(0))
            load_piece(0)
            a_bc = y[:, :, :]
            sp.dma_start(a_bc[:, 0, :], bc(a_self.rearrange("h u -> (h u)"), D)).then_inc(s_small, 16)
            sp.dma_start(a_bc[:, 1, :], bc(a_neigh.rearrange("h u -> (h u)"), D)).then_inc(s_small, 16)
            sp.dma_start(b0_bc[:, :], bc(b0.rearrange("h u -> (h u)"), D)).then_inc(s_small, 16)
            sp.dma_start(b1_bc[:, :], bc(b1, DH)).then_inc(s_small, 16)
            sp.dma_start(b2_bc[:, :], bc(b2, D)).then_inc(s_small, 16)
            sp.dma_start(gamma_sb[:, :], gammaT).then_inc(s_small, 16)
            sp.dma_start(beta_sb[:, :], betaT).then_inc(s_small, 16)
            load_piece(1)
            for g in range(1, 4):
                load(Graph(g))
            for n in range(2, len(PIECES)):
                load_piece(n)

            def turn(t):
                g = t.plus(-1)
                if g.within(NG):
                    sp.wait_ge(s_y_sb, g.count())
                    n = g.base if g.loop is None else g.loop * UNROLL + g.base
                    sp.dma_start(out[bass.ds(n, 1), :, :].rearrange("a p d -> p (a d)"), y[:, g.slot(2), :]).then_inc(s_out[g.slot(2)], 16)
                g = t.plus(4)
                if g.within(NG) and (g.loop is not None or g.base >= 4):
                    load(g)

            turns(sp, turn, NG)
            for i in range(2):
                sp.wait_ge(s_out[i], 16 * (NG // 2))

        @block.gpsimd
        def _(pool):
            nc.gpsimd.memset(ones[:, :], 1.0).then_inc(k_ones, 1)
            nc.gpsimd.memset(ident[:, :], 0.0).then_inc(k_ones, 1)
            nc.gpsimd.memset(head_sel[:, :, :], 0.0).then_inc(k_ones, 1)
            nc.gpsimd.memset(lo_rows8[:, :], 0.0).then_inc(k_ones, 1)
            nc.gpsimd.memset(halfpow[:, :], -0.5).then_inc(k_ones, 1)
            nc.gpsimd.memset(eps[:, :], EPS).then_inc(k_ones, 1)
            nc.gpsimd.memset(feats[:, :, :, UN:UE], 1.0).then_inc(k_ones, 1)
            pool.wait_ge(k_ones, 7)
            nc.gpsimd.affine_select(out=ident[:, :], in_=ident[:, :], compare_op=ALU.not_equal, fill=1.0,
                                    base=0, pattern=[[-1, P]], channel_multiplier=1).then_inc(k_const, 1)
            done = 7
            for first in (0, HEADS, 32, 32 + HEADS):
                pool.wait_ge(k_ones, done)
                nc.gpsimd.affine_select(out=head_sel[:, :, :], in_=head_sel[:, :, :], compare_op=ALU.not_equal,
                                        fill=1.0, base=-first, pattern=[[-1, HEADS], [0, N]],
                                        channel_multiplier=1).then_inc(k_ones, 1)
                done += 1
                if first in (HEADS, 32 + HEADS):
                    pool.wait_ge(k_ones, done)
                    nc.gpsimd.affine_select(out=lo_rows8[:, :], in_=lo_rows8[:, :], compare_op=ALU.not_equal,
                                            fill=-1.0, base=-first, pattern=[[-1, HEADS]],
                                            channel_multiplier=1).then_inc(k_ones, 1)
                    done += 1
            pool.wait_ge(k_ones, done)
            pool.wait_ge(k_const, 1)
            nc.gpsimd.tensor_copy(en_rhs[:, :, :], head_sel[:, :, :]).then_inc(k_const, 1)
            nc.gpsimd.tensor_copy(es_lhs[:, :], ones[0:64, :]).then_inc(k_const, 1)
            nc.gpsimd.tensor_copy(ident_r[:, :], ident[:, :]).then_inc(k_const, 1)
            pool.wait_ge(k_const, 4)

            def rstd(mv, ve, rs, s_mv, s_ve, s_rs, g, s_free):
                pool.wait_ge(s_mv, g.count())
                nc.gpsimd.tensor_tensor(ve[:, :], mv[:, 1:2], eps[:, :], ALU.add).then_inc(s_ve, 1)
                pool.wait_ge(s_ve, g.count())
                if g.has(1):
                    pool.wait_ge(s_free, g.count(1))
                nc.gpsimd.tensor_tensor(rs[:, :], ve[:, :], halfpow[:, :], ALU.pow).then_inc(s_rs, 1)

            def turn(t):
                g = t.plus(3)
                if g.within(NG):
                    rstd(mv0, ve0, rs0, s_mv0, s_ve0, s_rs0, g, s_xn)
                g = t
                if g.within(NG):
                    rstd(mv2, ve2, rs2, s_mv2, s_ve2, s_rs2, g, s_z)
                g = t.plus(1)
                if g.within(NG):
                    rstd(mv1, ve1, rs1, s_mv1, s_ve1, s_rs1, g, s_h)
                g = t.plus(2)
                if g.within(NG):
                    pool.wait_ge(s_en_parts, g.count())
                    if t.plus(1).within(NG) and t.plus(1).has(0):
                        pool.wait_ge(s_rs1, t.plus(1).count())
                    else:
                        pool.wait_ge(s_rs0, t.plus(3).count())
                    if g.has(1):
                        pool.wait_ge(s_scores, g.count(1))
                    nc.gpsimd.tensor_tensor(en_rhs[32:64, :, :],
                                            en_parts[32:64, :].unsqueeze(1).broadcast_to([32, HEADS, N]),
                                            head_sel[32:64, :, :], ALU.mult).then_inc(s_en_rhs, 1)
                    pool.wait_ge(s_en_rhs, g.count())
                    pool.wait_ge(s_inv, g.count())
                    if g.has(1):
                        pool.wait_ge(s_G, g.count(1))
                    nc.gpsimd.tensor_tensor(beT[:, :], inc[:, g.slot(2), 1, :],
                                            inv[:, g.slot(4), 0:1].broadcast_to([P, N]), ALU.mult).then_inc(s_beT, 1)
                g = t.plus(1)
                if g.within(NG):
                    s = g.slot(2)
                    if g.has(2):
                        pool.wait_ge(s_y_sb, g.count(2))
                    pool.wait_ge(s_h, g.count())
                    pool.wait_ge(s_x1, g.count())
                    nc.gpsimd.tensor_tensor(rest[:, s, :], x1[:, s, :], h[:, s, :], ALU.add).then_inc(s_xh, 1)
                    if g.base == 0:
                        pool.wait_ge(s_small, SMALL * 16)
                    pool.wait_ge(s_xh, g.count())
                    nc.gpsimd.tensor_tensor(rest[:, s, :], rest[:, s, :], b2_bc[:, :], ALU.add).then_inc(s_rest, 1)

            turns(pool, turn, NG)

        @block.scalar
        def _(act):
            for n, (_, hi, _) in enumerate(PIECES):
                if n < 3:
                    act.wait_ge(s_stage[n % 2], 16 * (n // 2 + 1))
                else:
                    if n == 3:
                        act.wait_ge(k_mean, 1)
                        nc.scalar.activation(z[:, :], p_w1a[:, :], ACT.Copy, scale=1.0 / DH).then_inc(k_mean_sb, 1)
                        act.wait_ge(k_t, 1)
                        nc.scalar.activation(t_bc[:, :], p_w1b[:, :], ACT.Copy).then_inc(k_mean_sb, 1)
                    act.wait_ge(k_cent, n - 2)
                nc.scalar.activation(hi, piece(n), ACT.Copy).then_inc(k_hi, 1)
                if n == 0:
                    act.wait_ge(k_wa, 4)
                    nc.scalar.activation(Wa_hi[:, :, :], wa_raw, ACT.Copy).then_inc(k_wa_hi, 1)

            def turn(t):
                g = t.plus(2)
                if g.within(NG):
                    act.wait_ge(s_xnT, g.count())
                    if g.has(1):
                        act.wait_ge(s_feats, g.count(1))
                    nc.scalar.activation(h0_hi[:, :], p_ta[:, :], ACT.Relu).then_inc(s_h0_hi, 1)
                g = t.plus(1)
                if g.within(NG):
                    act.wait_ge(s_max, g.count())
                    for i in range(HEADS):
                        last = nc.scalar.activation(att[:, i, :], att[:, i, :], ACT.Exp, bias=neg_max[:, i:i + 1])
                    last.then_inc(s_exp, 1)
                g = t
                if g.within(NG):
                    act.wait_ge(s_pre, g.count(per=2) - 1)
                    nc.scalar.activation(r[:, 0:HALF], r[:, 0:HALF], ACT.Relu).then_inc(s_r, 1)
                    act.wait_ge(s_rT, g.count(per=2) - 1)
                    if g.has(1):
                        act.wait_ge(s_w2, g.count(1))
                    nc.scalar.activation(rT_hi[:, 0:HALF], p_ta[:, :], ACT.Copy).then_inc(s_rT_hi, 1)
                g = t.plus(1)
                if g.within(NG):
                    act.wait_ge(s_attT, g.count())
                    if g.has(1):
                        act.wait_ge(s_o, g.count(1))
                    nc.scalar.activation(attT[:, :, :].rearrange("p h n -> p (h n)"), p_att[:, :],
                                         ACT.Copy).then_inc(s_attT_sb, 1)
                g = t
                if g.within(NG):
                    act.wait_ge(s_pre, g.count(per=2))
                    nc.scalar.activation(r[:, HALF:DH], r[:, HALF:DH], ACT.Relu).then_inc(s_r, 1)
                g = t.plus(2)
                if g.within(NG):
                    act.wait_ge(s_feats, g.count())
                    if g.has(1):
                        act.wait_ge(s_eT, g.count(1))
                    nc.scalar.activation(e_sb[:, :], p_e, ACT.Copy).then_inc(s_e_sb, 1)
                g = t
                if g.within(NG):
                    act.wait_ge(s_rT, g.count(per=2))
                    nc.scalar.activation(rT_hi[:, HALF:DH], p_tb[:, :], ACT.Copy).then_inc(s_rT_hi, 1)
                g = t.plus(1)
                if g.within(NG):
                    act.wait_ge(s_nb1, g.count())
                    if g.has(2):
                        act.wait_ge(s_hg, g.count(2))
                        act.wait_ge(s_xh, g.count(2))
                    nc.scalar.activation(h[:, g.slot(2), :], x1[:, g.slot(2), :], ACT.Relu, bias=nb1[:, :],
                                         scale=rs1[:, :]).then_inc(s_h, 1)
                    act.wait_ge(s_hg, g.count())
                    if g.has(1):
                        act.wait_ge(s_w1, g.count(1, per=2))
                    nc.scalar.activation(hg_hi[:, :], p_w1b[:, :], ACT.Copy).then_inc(s_hg_hi, 1)
                g = t.plus(2)
                if g.within(NG):
                    act.wait_ge(s_scores, g.count())
                    if g.has(1):
                        act.wait_ge(s_attT, g.count(1))
                    nc.scalar.activation(att[:, :, :].rearrange("p h n -> p (h n)"), p_scores, ACT.Copy,
                                         scale=SLOPE).then_inc(s_sloped, 1)
                    act.wait_ge(s_G, g.count())
                    if g.has(4):
                        act.wait_ge(s_y, g.count(4))
                    nc.scalar.activation(G[:, g.slot(4), :], p_G, ACT.Copy).then_inc(s_G_sb, 1)

            turns(act, turn, NG)



        @block.vector
        def _(dve):
            nc.vector.memset(wa_raw, 0.0).then_inc(k_cols, 1)
            dve.wait_ge(k_cols, 1)
            dve.wait_ge(s_stage[0], 16)
            dve.wait_ge(s_small, SMALL * 16)
            cols = 1
            for a, first in ((0, 0), (1, 32)):
                for c in range(DC):
                    s = c % 2
                    part = prod[:, s * D:(s + 1) * D]
                    nc.vector.tensor_tensor(part, piece(0)[:, c, :], y[:, a, :], ALU.mult).then_inc(k_cols, 1)
                    cols += 1
                    dve.wait_ge(k_cols, cols)
                    nc.vector.reduce_sum(wa_raw[:, c, first:first + HEADS],
                                         part.rearrange("p (h u) -> p h u", u=UN), X).then_inc(k_cols, 1)
                    cols += 1
                dve.wait_ge(k_cols, cols)
                nc.vector.tensor_copy(wa_raw[:, :, first + HEADS:first + 2 * HEADS],
                                      wa_raw[:, :, first:first + HEADS]).then_inc(k_wa, 2)
            dve.wait_ge(k_wa, 4)
            dve.wait_ge(k_wa_hi, 1)
            nc.vector.tensor_tensor(Wa_lo[:, :, :], wa_raw, Wa_hi[:, :, :], ALU.subtract).then_inc(k_wa_lo, 1)
            dve.wait_ge(k_ones, 13)
            nc.vector.reduce_sum(lo_rows[:, :], lo_rows8[:, :], X).then_inc(k_lorow, 1)
            dve.wait_ge(k_lorow, 1)
            for n, (_, hi, lo) in enumerate(PIECES):
                if n == 3:
                    dve.wait_ge(k_mean_sb, 2)
                    for m in (3, 4):
                        for c in range(CB):
                            g = nc.vector.scalar_tensor_tensor(
                                piece(m)[:, c, :], piece(m)[:, c, :], gamma_sb[:, (m - 3) * CB + c:(m - 3) * CB + c + 1],
                                z[:, :], ALU.mult, ALU.subtract)
                            if c == CB - 1:
                                g.then_inc(k_cent, 1)
                    dve.wait_ge(k_cent, 2)
                dve.wait_ge(k_hi, n + 1)
                nc.vector.tensor_tensor(lo, piece(n), hi, ALU.subtract).then_inc(k_lo, 1)

            def turn(t):
                g = t.plus(1)
                if g.within(NG):
                    att_flat = att[:, :, :].rearrange("p h n -> p (h n)")
                    dve.wait_ge(s_sloped, g.count())
                    nc.vector.tensor_tensor(att_flat, p_scores, att_flat, ALU.max).then_inc(s_leaky, 1)
                    dve.wait_ge(s_leaky, g.count())
                    nc.vector.reduce_max(neg_max[:, :], att[:, :, :], X, negate=True).then_inc(s_max, 1)
                g = t.plus(2)
                if g.within(NG):
                    dve.wait_ge(s_h0_hi, g.count())
                    nc.vector.scalar_tensor_tensor(h0_lo[:, :], p_ta[:, :], 0.0, h0_hi[:, :],
                                                   ALU.max, ALU.subtract).then_inc(s_h0_lo, 1)
                g = t
                if g.within(NG):
                    dve.wait_ge(s_w1, g.count(per=2) - 1)
                    if g.has(1):
                        dve.wait_ge(s_rT, g.count(1, per=2))
                    nc.vector.scalar_tensor_tensor(r[:, 0:HALF], p_w1a[:, :], inv[:, g.slot(4), 1:2],
                                                   b1_bc[:, 0:HALF], ALU.mult, ALU.add).then_inc(s_pre, 1)
                g = t.plus(-1)
                if g.within(NG):
                    dve.wait_ge(s_y, g.count())
                    dve.wait_ge(s_rest, g.count())
                    if g.has(2):
                        dve.wait_ge(s_out[g.slot(2)], g.plus(-2).uses(2, 16))
                    nc.vector.scalar_tensor_tensor(y[:, g.slot(2), :], p_tb[:, :], inv[:, g.slot(4), 1:2],
                                                   rest[:, g.slot(2), :], ALU.mult, ALU.add).then_inc(s_y_sb, 1)
                g = t
                if g.within(NG):
                    dve.wait_ge(s_r, g.count(per=2) - 1)
                    nc.vector.bn_stats(st2[:, 0, :], r[:, 0:HALF]).then_inc(s_stats2, 1)
                g = t.plus(3)
                if g.within(NG):
                    dve.wait_ge(s_in[g.slot(4)], g.uses(4, 32))
                    nc.vector.bn_stats(st0[:, :], x_in[:, g.slot(4), :]).then_inc(s_stats0, 1)
                    dve.wait_ge(s_stats0, g.count())
                g = t
                if g.within(NG):
                    dve.wait_ge(s_w1, g.count(per=2))
                    nc.vector.scalar_tensor_tensor(r[:, HALF:DH], p_w1b[:, :], inv[:, g.slot(4), 1:2],
                                                   b1_bc[:, HALF:DH], ALU.mult, ALU.add).then_inc(s_pre, 1)
                g = t.plus(3)
                if g.within(NG):
                    nc.vector.bn_aggr(mv0[:, :], st0[:, :]).then_inc(s_mv0, 1)
                    dve.wait_ge(s_rs0, g.count())
                    dve.wait_ge(s_mv0, g.count())
                    if g.has(1):
                        dve.wait_ge(s_xnT, g.count(1))
                    nc.vector.tensor_scalar(xn[:, :], x_in[:, g.slot(4), :], mv0[:, 0:1], rs0[:, :],
                                            ALU.subtract, ALU.mult).then_inc(s_xn, 1)
                g = t
                if g.within(NG):
                    dve.wait_ge(s_rT_hi, g.count(per=2) - 1)
                    nc.vector.tensor_tensor(rT_lo[:, 0:HALF], p_ta[:, :], rT_hi[:, 0:HALF],
                                            ALU.subtract).then_inc(s_rT_lo, 1)
                    dve.wait_ge(s_r, g.count(per=2))
                    nc.vector.bn_stats(st2[:, 1, :], r[:, HALF:DH]).then_inc(s_stats2, 1)
                    dve.wait_ge(s_stats2, g.count(per=2))
                g = t.plus(2)
                if g.within(NG):
                    dve.wait_ge(s_in[g.slot(4)], g.uses(4, 32))
                    if g.has(2):
                        dve.wait_ge(s_G, g.count(2))
                        dve.wait_ge(s_beT, g.count(2))
                    nc.vector.tensor_scalar(inc[:, g.slot(2), :, :], adj_in[:, g.slot(4), :, :], 0.0, None,
                                            ALU.not_equal).then_inc(s_inc, 1)
                if t.within(NG):
                    nc.vector.bn_aggr(mv2[:, :], st2[:, :, :].rearrange("p a b -> p (a b)")).then_inc(s_mv2, 1)
                if g.within(NG):
                    if g.has(1):
                        dve.wait_ge(s_scores, g.count(1))
                    nc.vector.tensor_scalar(mask[:, :], adj_in[:, g.slot(4), 0, :], -1.0, -NEG_BIG / SLOPE,
                                            ALU.add, ALU.mult).then_inc(s_mask, 1)
                    dve.wait_ge(s_feats, g.count())
                    if g.has(2):
                        dve.wait_ge(s_o, g.count(2))
                    nc.vector.tensor_tensor(feats[:, g.slot(2), :, 0:UN],
                                            p_f[:, :].rearrange("p (h u) -> p h u", u=UN),
                                            b0_bc[:, :].rearrange("p (h u) -> p h u", u=UN),
                                            ALU.add).then_inc(s_feats_sb, 1)
                g = t.plus(1)
                if g.within(NG):
                    s = g.slot(2)
                    dve.wait_ge(s_o, g.count())
                    nc.vector.reciprocal(rden[:, :].rearrange("p (b h) -> p b h", b=2), p_o[:, :, :, UN]).then_inc(s_rden, 1)
                    dve.wait_ge(s_rden, g.count())
                    nc.vector.tensor_tensor(o_sc[:, :].rearrange("p (b h u) -> p b h u", b=2, u=UN),
                                            p_o[:, :, :, 0:UN],
                                            rden[:, :].rearrange("p (b h) -> p b h", b=2).unsqueeze(3).broadcast_to([P, 2, HH, UN]),
                                            ALU.mult).then_inc(s_osc, 1)
                    dve.wait_ge(s_osc, g.count())
                    if g.has(2):
                        dve.wait_ge(s_xh, g.count(2))
                    nc.vector.scalar_tensor_tensor(x1[:, s, :], o_sc[:, :], 0.0, x_in[:, g.slot(4), :],
                                                   ALU.max, ALU.add).then_inc(s_x1, 1)
                    dve.wait_ge(s_x1, g.count())
                    nc.vector.bn_stats(st1[:, :], x1[:, s, :]).then_inc(s_stats1, 1)
                    dve.wait_ge(s_stats1, g.count())
                g = t
                if g.within(NG):
                    dve.wait_ge(s_rT_hi, g.count(per=2))
                    nc.vector.tensor_tensor(rT_lo[:, HALF:DH], p_tb[:, :], rT_hi[:, HALF:DH],
                                            ALU.subtract).then_inc(s_rT_lo, 1)
                g = t.plus(1)
                if g.within(NG):
                    nc.vector.bn_aggr(mv1[:, :], st1[:, :]).then_inc(s_mv1, 1)
                    dve.wait_ge(s_rs1, g.count())
                    dve.wait_ge(s_mv1, g.count())
                    if g.has(1):
                        dve.wait_ge(s_h, g.count(1))
                    nc.vector.tensor_scalar(nb1[:, :], mv1[:, 0:1], rs1[:, :], -1.0,
                                            ALU.mult, ALU.mult).then_inc(s_nb1, 1)
                g = t.plus(2)
                if g.within(NG):
                    dve.wait_ge(s_eT, g.count())
                    nc.vector.tensor_copy(e_hi[:, :], p_eT).then_inc(s_e_hi, 1)
                    dve.wait_ge(s_e_hi, g.count())
                    if g.has(1):
                        dve.wait_ge(s_scores, g.count(1))
                        dve.wait_ge(s_en_rhs, g.count(1))
                    nc.vector.scalar_tensor_tensor(en_parts[32:64, :], e_hi[32:64, :], lo_rows[32:64, :], p_s[32:64, 64:192],
                                                   ALU.mult, ALU.add).then_inc(s_en_parts, 1)
                    nc.vector.scalar_tensor_tensor(es_lhs[0:32, :], e_hi[0:32, :], lo_rows[0:32, :], p_s[0:32, 64:192],
                                                   ALU.mult, ALU.add).then_inc(s_es_lhs, 1)
                    dve.wait_ge(s_cnt, g.count())
                    nc.vector.tensor_scalar(cnt[:, :], p_cnt, TINY, None, ALU.max).then_inc(s_cnt1, 1)
                    dve.wait_ge(s_cnt1, g.count())
                    nc.vector.reciprocal(inv0[:, :], cnt[:, :]).then_inc(s_inv0, 1)
                    dve.wait_ge(s_inv0, g.count())
                    if g.has(4):
                        dve.wait_ge(s_beT, g.count(4))
                    nc.vector.scalar_tensor_tensor(inv[:, g.slot(4), :], p_cnt, 0.0, inv0[:, :],
                                                   ALU.is_gt, ALU.mult).then_inc(s_inv, 1)
                g = t
                if g.within(NG):
                    dve.wait_ge(s_w2, g.count())
                    dve.wait_ge(s_rs2, g.count())
                    if g.has(1):
                        dve.wait_ge(s_y, g.count(1))
                    nc.vector.scalar_tensor_tensor(z[:, :], p_w1a[:, :], rs2[:, :], t_bc[:, :],
                                                   ALU.mult, ALU.add).then_inc(s_z, 1)
                g = t.plus(1)
                if g.within(NG):
                    dve.wait_ge(s_hg_hi, g.count())
                    nc.vector.tensor_tensor(hg_lo[:, :], p_w1b[:, :], hg_hi[:, :], ALU.subtract).then_inc(s_hg_lo, 1)

            turns(dve, turn, NG)

        @block.tensor
        def _(pe):
            mm = nc.tensor.matmul
            pe.wait_ge(s_small, SMALL * 16)
            pe.wait_ge(s_stage[1], 32)
            pe.wait_ge(s_stage[0], 48)
            for vec, dst, s in ((gamma_sb, p_w1a, k_mean), (beta_sb, p_w1b, k_t)):
                for c in range(HC):
                    last = mm(dst[:, :], vec[:, c:c + 1].broadcast_to([P, P]), piece(3 + c // CB)[:, c % CB, :],
                              start=c == 0, stop=c == HC - 1)
                last.then_inc(s, 1)
            pe.wait_ge(k_const, 4)
            pe.wait_ge(k_wa_lo, 1)
            pe.wait_ge(k_lo, len(PIECES))
            pe.wait_ge(k_mean_sb, 2)

            def three(dst, hi, lo, w_hi, w_lo, first, final):
                mm(dst, hi, w_hi, start=first, stop=False)
                mm(dst, hi, w_lo, start=False, stop=False)
                return mm(dst, lo, w_hi, start=False, stop=final)

            def hidden(g, half, dst):
                for c in range(DC):
                    k = slice(c * P, (c + 1) * P)
                    n = slice(half * HALF, (half + 1) * HALF)
                    last = three(dst[:, :], hg_hi[:, k], hg_lo[:, k], W1_hi[:, c, n], W1_lo[:, c, n], c == 0, c == DC - 1)
                last.then_inc(s_w1, 1)

            def transposes(dst, src, s):
                for c in range(HALF // P):
                    last = nc.tensor.transpose(dst[:, c * P:(c + 1) * P], src[:, c * P:(c + 1) * P], ident[:, :])
                last.then_inc(s, 1)

            def turn(t):
                g = t
                if g.within(NG):
                    pe.wait_ge(s_hg_lo, g.count())
                    if g.has(1):
                        pe.wait_ge(s_z, g.count(1))
                    hidden(g, 0, p_w1a)
                    hidden(g, 1, p_w1b)
                g = t.plus(1)
                if g.within(NG):
                    pe.wait_ge(s_exp, g.count())
                    for i in range(HEADS):
                        last = nc.tensor.transpose(p_att[:, i * N:(i + 1) * N], att[:, i, :], ident[:, :])
                    last.then_inc(s_attT, 1)
                g = t
                if g.within(NG):
                    pe.wait_ge(s_r, g.count(per=2) - 1)
                    if g.plus(2).within(NG):
                        pe.wait_ge(s_h0_lo, g.plus(2).count())
                    transposes(p_ta, r[:, 0:HALF], s_rT)
                g = t.plus(2)
                if g.within(NG):
                    pe.wait_ge(s_h0_lo, g.count())
                    if g.has(1):
                        pe.wait_ge(s_feats_sb, g.count(1))
                        pe.wait_ge(s_e_sb, g.count(1))
                    for c in range(DC):
                        k = slice(c * P, (c + 1) * P)
                        three(p_f[:, :], h0_hi[:, k], h0_lo[:, k], W0_hi[:, c, :], W0_lo[:, c, :], c == 0, c == DC - 1)
                    for c in range(DC):
                        k = slice(c * P, (c + 1) * P)
                        last = three(p_e, h0_hi[:, k], h0_lo[:, k], Wa_hi[:, c, :], Wa_lo[:, c, :], c == 0, c == DC - 1)
                    last.then_inc(s_feats, 1)
                g = t.plus(1)
                if g.within(NG):
                    pe.wait_ge(s_attT_sb, g.count())
                    pe.wait_ge(s_feats_sb, g.count())
                    for i in range(HEADS):
                        last = mm(p_o[:, i // HH, i % HH, :], attT[:, i, :], feats[:, g.slot(2), i, :], start=True, stop=True)
                    last.then_inc(s_o, 1)
                g = t
                if g.within(NG):
                    pe.wait_ge(s_r, g.count(per=2))
                    if g.has(1):
                        pe.wait_ge(s_y_sb, g.count(1))
                    transposes(p_tb, r[:, HALF:DH], s_rT)
                g = t.plus(2)
                if g.within(NG):
                    pe.wait_ge(s_e_sb, g.count())
                    if g.has(1):
                        pe.wait_ge(s_es_lhs, g.count(1))
                        pe.wait_ge(s_inv, g.count(1))
                    pe.wait_ge(s_inc, g.count())
                    mm(p_cnt[:, 0:1], inc[:, g.slot(2), 0, :], ones[:, 0:1], start=True, stop=True)
                    mm(p_cnt[:, 1:2], inc[:, g.slot(2), 1, :], adj_in[:, g.slot(4), 1, 0:1], start=True,
                       stop=True).then_inc(s_cnt, 1)
                    nc.tensor.transpose(p_eT, e_sb[:, :], ident[:, :]).then_inc(s_eT, 1)
                g = t
                if g.within(NG):
                    for c in range(HC):
                        if c % CB == 0:
                            pe.wait_ge(s_rT_lo, g.count(per=2) - 1 + c // CB)
                        k = slice(c * P, (c + 1) * P)
                        last = three(p_w1a[:, :], rT_hi[:, k], rT_lo[:, k], W2_hi[:, c, :], W2_lo[:, c, :], c == 0, c == HC - 1)
                    last.then_inc(s_w2, 1)
                g = t.plus(1)
                if g.within(NG):
                    pe.wait_ge(s_h, g.count())
                    pe.wait_ge(s_G_sb, g.count())
                    if g.has(1):
                        pe.wait_ge(s_pre, g.count(1, per=2))
                    for c in range(DC):
                        last = mm(p_w1b[:, c * P:(c + 1) * P], h[:, g.slot(2), c * P:(c + 1) * P], G[:, g.slot(4), :],
                                  start=True, stop=True)
                    last.then_inc(s_hg, 1)
                g = t.plus(2)
                if g.within(NG):
                    pe.wait_ge(s_en_rhs, g.count())
                    pe.wait_ge(s_es_lhs, g.count())
                    pe.wait_ge(s_mask, g.count())
                    if g.has(1):
                        pe.wait_ge(s_osc, g.count(1))
                    for b in range(2):
                        dst = p_att[:, b * HALF:(b + 1) * HALF]
                        mm(dst, es_lhs[:, :], en_rhs[:, b * HH:(b + 1) * HH, :].rearrange("p h n -> p (h n)"),
                           start=True, stop=False)
                        last = mm(dst.rearrange("p (h n) -> p h n", n=N), ident_r[:, :],
                                  mask[:, :].unsqueeze(1).broadcast_to([P, HH, N]), start=False, stop=True)
                    last.then_inc(s_scores, 1)
                    pe.wait_ge(s_beT, g.count())
                    if g.has(1):
                        pe.wait_ge(s_G_sb, g.count(1))
                    mm(p_G, inc[:, g.slot(2), 1, :], beT[:, :], start=True, stop=True).then_inc(s_G, 1)
                g = t.plus(3)
                if g.within(NG):
                    pe.wait_ge(s_xn, g.count())
                    if t.within(NG):
                        pe.wait_ge(s_rT_lo, t.count(per=2) - 1)
                    elif g.has(1):
                        pe.wait_ge(s_h0_lo, g.count(1))
                    transposes(p_ta, xn, s_xnT)
                g = t
                if g.within(NG):
                    pe.wait_ge(s_z, g.count())
                    pe.wait_ge(s_rT_lo, g.count(per=2))
                    mm(p_tb[:, :], G[:, g.slot(4), :], z[:, :], start=True, stop=True).then_inc(s_y, 1)

            turns(pe, turn, NG)


_INS = ["x", "adj2", "W0T", "b0", "a_self", "a_neigh", "W1T", "b1", "gammaT", "betaT", "W2T", "b2"]


def kernel(x, adj, L0_gnn_W, L0_gnn_b, L0_gnn_a_self, L0_gnn_a_neigh, L1_gnn_W1, L1_gnn_b1, L1_gnn_gamma,
           L1_gnn_beta, L1_gnn_W2, L1_gnn_b2):
    import numpy as np
    import concourse.bacc as bacc
    from concourse.bass_utils import run_bass_kernel_spmd

    adj = np.asarray(adj)
    f = np.asarray(L0_gnn_W).shape[1]
    laid = {
        "x": x,
        "adj2": np.stack([adj, adj.transpose(0, 2, 1)], axis=2),
        "W0T": np.asarray(L0_gnn_W).transpose(1, 0, 2).reshape(f, -1),
        "b0": L0_gnn_b, "a_self": L0_gnn_a_self, "a_neigh": L0_gnn_a_neigh,
        "W1T": np.asarray(L1_gnn_W1).T, "b1": L1_gnn_b1,
        "gammaT": np.asarray(L1_gnn_gamma).reshape(-1, P).T, "betaT": np.asarray(L1_gnn_beta).reshape(-1, P).T,
        "W2T": np.asarray(L1_gnn_W2).T, "b2": L1_gnn_b2,
    }
    nc = bacc.Bacc("TRN2", target_bir_lowering=False, num_devices=1)
    arrays, args = {}, []
    for name in _INS:
        a = np.ascontiguousarray(laid[name])
        arrays[f"in_{name}"] = a
        args.append(nc.dram_tensor(f"in_{name}", a.shape, mybir.dt.from_np(a.dtype), kind="ExternalInput").ap())
    out = nc.dram_tensor("out", arrays["in_x"].shape, F32, kind="ExternalOutput").ap()
    gnn_two_layers(nc, *args, out)
    got = run_bass_kernel_spmd(nc, [arrays], core_ids=[0])
    return got.results[0]["out"]
```

```python
import concourse.bass as bass
from concourse import mybir
from contextlib import ExitStack

F32 = mybir.dt.float32
F32R = mybir.dt.float32r
ALU = mybir.AluOpType
ACT = mybir.ActivationFunctionType
X = mybir.AxisListType.X

P = 128
AHEAD = 3
UNROLL = 4
EPS = 1e-5
SLOPE = 0.2
NEG_BIG = -1e10
TINY = 1e-30


class Graph:

    def __init__(self, base, loop=None):
        self.base, self.loop = base, loop

    def plus(self, n):
        return Graph(self.base + n, self.loop)

    def within(self, total):
        return self.loop is not None or 0 <= self.base < total

    def slot(self, ring):
        return self.base % ring

    def has(self, back):
        return self.loop is not None or self.base >= back

    def count(self, back=0, per=1):
        n = (self.base + 1 - back) * per
        return n if self.loop is None else self.loop * (UNROLL * per) + n

    def uses(self, ring, per):
        n = (self.base // ring + 1) * per
        return n if self.loop is None else self.loop * (UNROLL // ring * per) + n


def turns(eng, turn, total, before={}):
    loops = (total - AHEAD - 2) // UNROLL
    for t in range(-AHEAD, 1):
        if t in before:
            before[t]()
        turn(Graph(t))
    with eng.Fori(0, loops) as k:
        for u in range(1, UNROLL + 1):
            turn(Graph(u, k))
    for t in range(1 + loops * UNROLL, total + 1):
        turn(Graph(t))


def gnn_two_layers(nc, x, adj2, W0T, b0, a_self, a_neigh, W1T, b1, gammaT, betaT, W2T, b2, out):
    NG, N, D = x.shape
    HEADS = a_self.shape[0]
    UN = D // HEADS
    DH = W1T.shape[1]
    DC, HC = D // P, DH // P
    HALF = 512
    HH = HEADS // 2
    CB = HC // 2
    UE = UN + 1
    HN = HEADS * N

    ctx = ExitStack()
    with ctx:
        def sb(name, shape, dt=F32):
            return ctx.enter_context(nc.sbuf_tensor(name, shape, dt))

        def sem(name):
            return ctx.enter_context(nc.semaphore(name))

        W0_hi, W0_lo = (sb(n, [P, DC, D], F32R) for n in ("W0_hi", "W0_lo"))
        Wa = sb("Wa", [P, DC, P], F32R)
        W1_hi, W1_lo = (sb(n, [P, DC, DH], F32R) for n in ("W1_hi", "W1_lo"))
        W2_hi, W2_lo = (sb(n, [P, HC, D], F32R) for n in ("W2_hi", "W2_lo"))
        stage = sb("stage", [P, 2, 4 * HALF])
        ident = sb("ident", [P, P])
        ones = sb("ones", [P, P])
        halfpow = sb("halfpow", [P, 1])
        eps = sb("eps", [P, 1])
        neg_one = sb("neg_one", [P, 1])
        neg_big = sb("neg_big", [P, 1])
        b0_bc = sb("b0_bc", [P, D])
        b1_bc = sb("b1_bc", [P, DH])
        b2_bc = sb("b2_bc", [P, D])
        t_bc = sb("t_bc", [P, D])
        gamma_sb = sb("gamma_sb", [P, HC])
        beta_sb = sb("beta_sb", [P, HC])
        head_sel = sb("head_sel", [64, HEADS, N])
        lo_rows8 = sb("lo_rows8", [64, HEADS])
        lo_rows = sb("lo_rows", [64, 1])
        x_in = sb("x_in", [P, 4, D])
        adj_in = sb("adj_in", [P, 4, 2, N])
        inc = sb("inc", [P, 2, 2, N])
        mask = sb("mask", [P, N])
        cnt = sb("cnt", [P, 2])
        inv0 = sb("inv0", [P, 2])
        inv = sb("inv", [P, 4, 2])
        beT = sb("beT", [P, N + 1])
        G = sb("G", [P, 4, N + 2])
        st0 = sb("st0", [P, 6])
        st1 = sb("st1", [P, 6])
        st2 = sb("st2", [P, 2, 6])
        mv0 = sb("mv0", [P, 2])
        mv1 = sb("mv1", [P, 2])
        mv2 = sb("mv2", [P, 2])
        ve0, ve1, ve2 = sb("ve0", [P, 1]), sb("ve1", [P, 1]), sb("ve2", [P, 1])
        rs0, rs1, rs2 = sb("rs0", [P, 1]), sb("rs1", [P, 1]), sb("rs2", [P, 1])
        nm0, nm1 = sb("nm0", [P, 1]), sb("nm1", [P, 1])
        nb0, nb1 = sb("nb0", [P, 1]), sb("nb1", [P, 1])
        xn = sb("xn", [P, D])
        h0 = sb("h0", [P, DC, 2, N], F32R)
        feats = sb("feats", [P, 2, HEADS, UE])
        e_hi = sb("e_hi", [64, N], F32R)
        e_rest = sb("e_rest", [64, N])
        en_parts = sb("en_parts", [64, N])
        es_lhs = sb("es_lhs", [64, N], F32R)
        en_rhs = sb("en_rhs", [64, HEADS, N], F32R)
        att = sb("att", [P, HEADS, N])
        neg_max = sb("neg_max", [P, HEADS])
        attT = sb("attT", [P, HEADS, N])
        rden = sb("rden", [P, HEADS])
        o_sc = sb("o_sc", [P, D])
        x1 = sb("x1", [P, 2, D])
        h = sb("h", [P, 2, D])
        rest = sb("rest", [P, 2, D])
        hg_hi, hg_lo = sb("hg_hi", [P, D], F32R), sb("hg_lo", [P, D], F32R)
        r = sb("r", [P, DH])
        rT_hi, rT_lo = sb("rT_hi", [P, DH], F32R), sb("rT_lo", [P, DH], F32R)
        z = sb("z", [P, D])
        y = sb("y", [P, 2, D])

        def bank(name, n=1):
            return ctx.enter_context(nc.psum_tensor(name, [P, n * HALF], F32))

        p_w1a = bank("p_w1a")
        p_w1b = bank("p_w1b")
        p_att = bank("p_att", 2)
        p_ta = bank("p_ta")
        p_tb = bank("p_tb")
        p_f = bank("p_f")
        p_s = bank("p_s")
        p_e = p_s[:, 0:2 * N]
        p_G = p_s[:, 2 * N:3 * N + 1]
        p_o = p_att[:, :].rearrange("p (b c) -> p b c", b=2)[:, :, 0:HH * UE].rearrange("p b (h u) -> p b h u", u=UE)

        s_in = [sem(f"s_in{i}") for i in range(4)]
        s_out = [sem(f"s_out{i}") for i in range(2)]
        s_small = sem("s_small")
        s_stage = [sem(f"s_stage{i}") for i in range(2)]
        k_hi, k_lo, k_const, k_ones = sem("k_hi"), sem("k_lo"), sem("k_const"), sem("k_ones")
        k_wa, k_cols = sem("k_wa"), sem("k_cols")
        k_mean, k_mean_sb, k_cent, k_t, k_lorow = sem("k_mean"), sem("k_mean_sb"), sem("k_cent"), sem("k_t"), sem("k_lorow")
        s_stats0, s_mv0, s_ve0, s_rs0, s_nm0, s_nb0, s_xn, s_xnT = (sem("s_" + n) for n in ("stats0", "mv0", "ve0", "rs0", "nm0", "nb0", "xn", "xnT"))
        s_h0_hi, s_h0_lo, s_feats, s_feats_sb = (sem("s_" + n) for n in ("h0_hi", "h0_lo", "feats", "feats_sb"))
        s_e_hi, s_e_rest, s_es_lhs, s_en_parts, s_en_rhs = (sem("s_" + n) for n in ("e_hi", "e_rest", "es_lhs", "en_parts", "en_rhs"))
        s_absent, s_mask, s_scores, s_sloped, s_leaky, s_masked, s_max = (sem("s_" + n) for n in ("absent", "mask", "scores", "sloped", "leaky", "masked", "max"))
        s_exp, s_attT, s_attT_sb, s_o, s_rden, s_osc, s_x1 = (sem("s_" + n) for n in ("exp", "attT", "attT_sb", "o", "rden", "osc", "x1"))
        s_inc, s_sizes, s_e, s_row, s_cnt1, s_inv0, s_inv, s_beT, s_G, s_G_sb = (sem("s_" + n) for n in ("inc", "sizes", "e", "row", "cnt1", "inv0", "inv", "beT", "G", "G_sb"))
        s_stats1, s_mv1, s_ve1, s_rs1, s_nm1, s_nb1, s_h, s_xh, s_rest = (sem("s_" + n) for n in ("stats1", "mv1", "ve1", "rs1", "nm1", "nb1", "h", "xh", "rest"))
        s_hg, s_hg_hi, s_hg_lo, s_w1, s_pre, s_r = (sem("s_" + n) for n in ("hg", "hg_hi", "hg_lo", "w1", "pre", "r"))
        s_stats2, s_mv2, s_ve2, s_rs2, s_rT, s_rT_hi, s_rT_lo = (sem("s_" + n) for n in ("stats2", "mv2", "ve2", "rs2", "rT", "rT_hi", "rT_lo"))
        s_w2, s_z, s_y, s_y_sb = (sem("s_" + n) for n in ("w2", "z", "y", "y_sb"))

        block = ctx.enter_context(nc.Block())

        def piece(n):
            return stage[:, n % 2, :].rearrange("p (c n) -> p c n", c=4)

        W0v, W1v, W2v = (w.rearrange("(c p) n -> p c n", p=P) for w in (W0T, W1T, W2T))
        PIECES = [
            (W0v, W0_hi[:, :, :], W0_lo[:, :, :]),
            (W2v[:, 0:CB, :], W2_hi[:, 0:CB, :], W2_lo[:, 0:CB, :]),
            (W2v[:, CB:HC, :], W2_hi[:, CB:HC, :], W2_lo[:, CB:HC, :]),
            (W1v[:, :, 0:HALF], W1_hi[:, :, 0:HALF], W1_lo[:, :, 0:HALF]),
            (W1v[:, :, HALF:DH], W1_hi[:, :, HALF:DH], W1_lo[:, :, HALF:DH]),
        ]
        SMALL = 7
        wa_raw = r[:, 0:2 * DC * HEADS].rearrange("p (a c n) -> p a c n", a=2, c=DC)
        prod = att[:, :, :].rearrange("p h n -> p (h n)")

        @block.sync
        def _(sp):
            def load(g):
                if g.has(4):
                    sp.wait_ge(s_x1, g.count(4))
                    sp.wait_ge(s_inc, g.count(4))
                    sp.wait_ge(s_mask, g.count(4))
                    sp.wait_ge(s_row, g.count(4))
                s = g.slot(4)
                n = g.base if g.loop is None else g.loop * UNROLL + g.base
                sp.dma_start(x_in[:, s, :], x[bass.ds(n, 1), :, :].rearrange("a p d -> p (a d)")).then_inc(s_in[s], 16)
                sp.dma_start(adj_in[:, s, :, :], adj2[bass.ds(n, 1), :, :, :].rearrange("a p t n -> p (a t) n")).then_inc(s_in[s], 16)

            def load_piece(n):
                if n >= 2:
                    sp.wait_ge(k_hi, n - 1)
                    sp.wait_ge(k_lo, n - 1)
                sp.dma_start(piece(n), PIECES[n][0]).then_inc(s_stage[n % 2], 16)

            def bc(v, n):
                return v.rearrange("(a n) -> a n", a=1).broadcast_to([P, n])

            load(Graph(0))
            load_piece(0)
            a_bc = y[:, :, :]
            sp.dma_start(a_bc[:, 0, :], bc(a_self.rearrange("h u -> (h u)"), D)).then_inc(s_small, 16)
            sp.dma_start(a_bc[:, 1, :], bc(a_neigh.rearrange("h u -> (h u)"), D)).then_inc(s_small, 16)
            sp.dma_start(b0_bc[:, :], bc(b0.rearrange("h u -> (h u)"), D)).then_inc(s_small, 16)
            sp.dma_start(b1_bc[:, :], bc(b1, DH)).then_inc(s_small, 16)
            sp.dma_start(b2_bc[:, :], bc(b2, D)).then_inc(s_small, 16)
            sp.dma_start(gamma_sb[:, :], gammaT).then_inc(s_small, 16)
            sp.dma_start(beta_sb[:, :], betaT).then_inc(s_small, 16)
            load_piece(1)
            for g in range(1, 4):
                load(Graph(g))
            for n in range(2, len(PIECES)):
                load_piece(n)

            def turn(t):
                g = t.plus(-1)
                if g.within(NG):
                    sp.wait_ge(s_y_sb, g.count())
                    n = g.base if g.loop is None else g.loop * UNROLL + g.base
                    sp.dma_start(out[bass.ds(n, 1), :, :].rearrange("a p d -> p (a d)"), y[:, g.slot(2), :]).then_inc(s_out[g.slot(2)], 16)
                g = t.plus(4)
                if g.within(NG) and (g.loop is not None or g.base >= 4):
                    load(g)

            turns(sp, turn, NG)
            for i in range(2):
                sp.wait_ge(s_out[i], 16 * (NG // 2))

        @block.gpsimd
        def _(pool):
            nc.gpsimd.memset(ones[:, :], 1.0).then_inc(k_ones, 1)
            nc.gpsimd.memset(ident[:, :], 0.0).then_inc(k_ones, 1)
            nc.gpsimd.memset(head_sel[:, :, :], 0.0).then_inc(k_ones, 1)
            nc.gpsimd.memset(lo_rows8[:, :], 0.0).then_inc(k_ones, 1)
            nc.gpsimd.memset(halfpow[:, :], -0.5).then_inc(k_ones, 1)
            nc.gpsimd.memset(eps[:, :], EPS).then_inc(k_ones, 1)
            nc.gpsimd.memset(neg_one[:, :], -1.0).then_inc(k_ones, 1)
            nc.gpsimd.memset(neg_big[:, :], NEG_BIG).then_inc(k_ones, 1)
            nc.gpsimd.memset(G[:, 3, N:N + 2], 1.0).then_inc(k_ones, 1)
            nc.gpsimd.memset(feats[:, :, :, UN:UE], 1.0).then_inc(k_ones, 1)
            pool.wait_ge(k_ones, 10)
            nc.gpsimd.affine_select(out=ident[:, :], in_=ident[:, :], compare_op=ALU.not_equal, fill=1.0,
                                    base=0, pattern=[[-1, P]], channel_multiplier=1).then_inc(k_const, 1)
            done = 10
            for first in (0, HEADS, 2 * HEADS, 32, 32 + HEADS, 32 + 2 * HEADS):
                pool.wait_ge(k_ones, done)
                nc.gpsimd.affine_select(out=head_sel[:, :, :], in_=head_sel[:, :, :], compare_op=ALU.not_equal,
                                        fill=1.0, base=-first, pattern=[[-1, HEADS], [0, N]],
                                        channel_multiplier=1).then_inc(k_ones, 1)
                done += 1
                if first in (HEADS, 32 + HEADS):
                    pool.wait_ge(k_ones, done)
                    nc.gpsimd.affine_select(out=lo_rows8[:, :], in_=lo_rows8[:, :], compare_op=ALU.not_equal,
                                            fill=1.0, base=-first, pattern=[[-1, HEADS]],
                                            channel_multiplier=1).then_inc(k_ones, 1)
                    done += 1
            pool.wait_ge(k_ones, done)
            pool.wait_ge(k_const, 1)
            nc.gpsimd.tensor_copy(en_rhs[:, :, :], head_sel[:, :, :]).then_inc(k_const, 1)
            nc.gpsimd.tensor_copy(es_lhs[:, :], ones[0:64, :]).then_inc(k_const, 1)
            pool.wait_ge(k_const, 3)

            def rstd(g, mv, ve, rs, s_mv, s_ve, s_rs, s_free, nm=None, s_nm=None):
                pool.wait_ge(s_mv, g.count())
                nc.gpsimd.tensor_tensor(ve[:, :], mv[:, 1:2], eps[:, :], ALU.add).then_inc(s_ve, 1)
                if g.has(1):
                    pool.wait_ge(s_free, g.count(1))
                if nm is not None:
                    nc.gpsimd.tensor_tensor(nm[:, :], mv[:, 0:1], neg_one[:, :], ALU.mult).then_inc(s_nm, 1)
                pool.wait_ge(s_ve, g.count())
                nc.gpsimd.tensor_tensor(rs[:, :], ve[:, :], halfpow[:, :], ALU.pow).then_inc(s_rs, 1)

            def shift(g, nm, rs, nb, s_nm, s_rs, s_nb):
                pool.wait_ge(s_nm, g.count())
                pool.wait_ge(s_rs, g.count())
                nc.gpsimd.tensor_tensor(nb[:, :], nm[:, :], rs[:, :], ALU.mult).then_inc(s_nb, 1)

            def turn(t):
                g = t.plus(3)
                if g.within(NG):
                    rstd(g, mv0, ve0, rs0, s_mv0, s_ve0, s_rs0, s_xn, nm0, s_nm0)
                    shift(g, nm0, rs0, nb0, s_nm0, s_rs0, s_nb0)
                g = t
                if g.within(NG):
                    rstd(g, mv2, ve2, rs2, s_mv2, s_ve2, s_rs2, s_z)
                g = t.plus(2)
                if g.within(NG):
                    pool.wait_ge(s_in[g.slot(4)], g.uses(4, 32))
                    if g.has(1):
                        pool.wait_ge(s_masked, g.count(1, per=2))
                    nc.gpsimd.tensor_tensor(mask[:, :], ones[:, :], adj_in[:, g.slot(4), 0, :], ALU.subtract).then_inc(s_absent, 1)
                    pool.wait_ge(s_absent, g.count())
                    nc.gpsimd.tensor_tensor(mask[:, :], mask[:, :], neg_big[:, :].broadcast_to([P, N]), ALU.mult).then_inc(s_mask, 1)
                    pool.wait_ge(s_en_parts, g.count())
                    pool.wait_ge(s_mask, g.count())
                    if g.has(1):
                        pool.wait_ge(s_scores, g.count(1, per=2))
                    nc.gpsimd.tensor_tensor(en_rhs[32:64, :, :],
                                            en_parts[32:64, :].unsqueeze(1).broadcast_to([32, HEADS, N]),
                                            head_sel[32:64, :, :], ALU.mult).then_inc(s_en_rhs, 1)
                g = t.plus(1)
                if g.within(NG):
                    if g.plus(1).within(NG):
                        pool.wait_ge(s_en_rhs, g.plus(1).count())
                    rstd(g, mv1, ve1, rs1, s_mv1, s_ve1, s_rs1, s_h, nm1, s_nm1)
                    shift(g, nm1, rs1, nb1, s_nm1, s_rs1, s_nb1)
                g = t.plus(2)
                if g.within(NG):
                    pool.wait_ge(s_en_rhs, g.count())
                    pool.wait_ge(s_inv, g.count())
                    if g.has(1):
                        pool.wait_ge(s_G, g.count(1))
                    nc.gpsimd.tensor_tensor(beT[:, 0:N], inc[:, g.slot(2), 1, :],
                                            inv[:, g.plus(-1).slot(4), 1:2].broadcast_to([P, N]), ALU.mult).then_inc(s_beT, 1)
                    nc.gpsimd.tensor_copy(beT[:, N:N + 1], adj_in[:, g.slot(4), 1, 0:1]).then_inc(s_row, 1)
                g = t.plus(1)
                if g.within(NG):
                    s = g.slot(2)
                    if g.has(2):
                        pool.wait_ge(s_y_sb, g.count(2))
                    pool.wait_ge(s_h, g.count())
                    pool.wait_ge(s_x1, g.count())
                    nc.gpsimd.tensor_tensor(rest[:, s, :], x1[:, s, :], h[:, s, :], ALU.add).then_inc(s_xh, 1)
                    if g.base == 0:
                        pool.wait_ge(s_small, SMALL * 16)
                    pool.wait_ge(s_xh, g.count())
                    nc.gpsimd.tensor_tensor(rest[:, s, :], rest[:, s, :], b2_bc[:, :], ALU.add).then_inc(s_rest, 1)

            turns(pool, turn, NG)

        @block.scalar
        def _(act):
            def rounded(n):
                if n in (1, 2):
                    act.wait_ge(k_cent, n)
                else:
                    act.wait_ge(s_stage[n % 2], 16 * (n // 2 + 1))
                nc.scalar.activation(PIECES[n][1], piece(n), ACT.Copy).then_inc(k_hi, 1)

            def setup_w2():
                act.wait_ge(k_mean, 1)
                nc.scalar.activation(z[:, :], p_w1a[:, :], ACT.Copy, scale=1.0 / DH).then_inc(k_mean_sb, 1)
                act.wait_ge(k_t, 1)
                nc.scalar.activation(t_bc[:, :], p_w1b[:, :], ACT.Copy).then_inc(k_mean_sb, 1)
                rounded(1)
                rounded(2)

            def setup_w1():
                rounded(3)
                rounded(4)

            rounded(0)

            def exps(g, half):
                act.wait_ge(s_max, g.count(per=2) - 1 + half)
                for i in range(half * HH, (half + 1) * HH):
                    last = nc.scalar.activation(att[:, i, :], att[:, i, :], ACT.Exp, bias=neg_max[:, i:i + 1])
                last.then_inc(s_exp, 1)

            def turn(t):
                g = t.plus(2)
                if g.within(NG):
                    act.wait_ge(s_xnT, g.count())
                    if g.has(1):
                        act.wait_ge(s_feats, g.count(1))
                    nc.scalar.activation(h0[:, :, 0, :], p_ta[:, :].rearrange("p (c n) -> p c n", n=N), ACT.Relu).then_inc(s_h0_hi, 1)
                g = t.plus(1)
                if g.within(NG):
                    exps(g, 0)
                g = t
                if g.within(NG):
                    act.wait_ge(s_pre, g.count(per=2) - 1)
                    nc.scalar.activation(r[:, 0:HALF], r[:, 0:HALF], ACT.Relu).then_inc(s_r, 1)
                if t.plus(1).within(NG):
                    exps(t.plus(1), 1)
                if g.within(NG):
                    act.wait_ge(s_rT, g.count(per=2) - 1)
                    if g.has(1):
                        act.wait_ge(s_w2, g.count(1))
                    nc.scalar.activation(rT_hi[:, 0:HALF], p_ta[:, :], ACT.Copy).then_inc(s_rT_hi, 1)
                g = t
                if g.within(NG):
                    act.wait_ge(s_pre, g.count(per=2))
                    nc.scalar.activation(r[:, HALF:DH], r[:, HALF:DH], ACT.Relu).then_inc(s_r, 1)
                g = t.plus(2)
                if g.within(NG):
                    act.wait_ge(s_e, g.count())
                    if g.has(1):
                        act.wait_ge(s_e_rest, g.count(1))
                    nc.scalar.activation(e_hi[:, :], p_e[0:64, 0:N], ACT.Copy).then_inc(s_e_hi, 1)
                g = t.plus(1)
                if g.within(NG):
                    act.wait_ge(s_attT, g.count())
                    if g.has(1):
                        act.wait_ge(s_o, g.count(1))
                    nc.scalar.activation(attT[:, :, :].rearrange("p h n -> p (h n)"), p_att[:, :],
                                         ACT.Copy).then_inc(s_attT_sb, 1)
                g = t.plus(3)
                if g.within(NG):
                    act.wait_ge(s_nb0, g.count())
                    if g.has(1):
                        act.wait_ge(s_xnT, g.count(1))
                    nc.scalar.activation(xn[:, :], x_in[:, g.slot(4), :], ACT.Identity, bias=nb0[:, :],
                                         scale=rs0[:, :]).then_inc(s_xn, 1)
                g = t
                if g.within(NG):
                    act.wait_ge(s_rT, g.count(per=2))
                    nc.scalar.activation(rT_hi[:, HALF:DH], p_tb[:, :], ACT.Copy).then_inc(s_rT_hi, 1)
                g = t.plus(1)
                if g.within(NG):
                    act.wait_ge(s_nb1, g.count())
                    if g.has(2):
                        act.wait_ge(s_hg, g.count(2))
                        act.wait_ge(s_xh, g.count(2))
                    nc.scalar.activation(h[:, g.slot(2), :], x1[:, g.slot(2), :], ACT.Relu, bias=nb1[:, :],
                                         scale=rs1[:, :]).then_inc(s_h, 1)
                    act.wait_ge(s_hg, g.count())
                    if g.has(1):
                        act.wait_ge(s_w1, g.count(1, per=2))
                    nc.scalar.activation(hg_hi[:, :], p_w1b[:, :], ACT.Copy).then_inc(s_hg_hi, 1)
                g = t.plus(2)
                if g.within(NG):
                    for b in range(2):
                        act.wait_ge(s_scores, g.count(per=2) - 1 + b)
                        if b == 0 and g.has(1):
                            act.wait_ge(s_attT, g.count(1))
                        nc.scalar.activation(att[:, b * HH:(b + 1) * HH, :].rearrange("p h n -> p (h n)"),
                                             p_att[:, b * HALF:(b + 1) * HALF], ACT.Copy, scale=SLOPE).then_inc(s_sloped, 1)
                    act.wait_ge(s_G, g.count())
                    if g.has(4):
                        act.wait_ge(s_y, g.count(4))
                    nc.scalar.activation(G[:, g.slot(4), 0:N + 1], p_G, ACT.Copy).then_inc(s_G_sb, 1)

            turns(act, turn, NG, {-1: setup_w2, 0: setup_w1})



        @block.vector
        def _(dve):
            nc.vector.memset(Wa[:, :, :].bitcast(F32), 0.0).then_inc(k_cols, 1)
            dve.wait_ge(s_stage[0], 16)
            dve.wait_ge(s_small, SMALL * 16)
            cols = 1
            for a in range(2):
                for c in range(DC):
                    part = prod[:, c % 2 * D:(c % 2 + 1) * D]
                    nc.vector.tensor_tensor(part, piece(0)[:, c, :], y[:, a, :], ALU.mult).then_inc(k_cols, 1)
                    cols += 1
                    dve.wait_ge(k_cols, cols)
                    nc.vector.reduce_sum(wa_raw[:, a, c, :], part.rearrange("p (h u) -> p h u", u=UN), X).then_inc(k_cols, 1)
                    cols += 1
            dve.wait_ge(k_cols, cols)
            for a in range(2):
                first = 32 * a
                for i in range(2):
                    nc.vector.tensor_copy(Wa[:, :, first + i * HEADS:first + (i + 1) * HEADS], wa_raw[:, a, :, :]).then_inc(k_wa, 1)
                dve.wait_ge(k_wa, 3 * a + 2)
                nc.vector.tensor_tensor(Wa[:, :, first + 2 * HEADS:first + 3 * HEADS], wa_raw[:, a, :, :],
                                        Wa[:, :, first:first + HEADS], ALU.subtract).then_inc(k_wa, 1)
            dve.wait_ge(k_ones, 18)
            nc.vector.reduce_sum(lo_rows[:, :], lo_rows8[:, :], X).then_inc(k_lorow, 1)
            dve.wait_ge(k_lorow, 1)

            def rest_of(n):
                dve.wait_ge(k_hi, n + 1)
                nc.vector.tensor_tensor(PIECES[n][2], piece(n), PIECES[n][1], ALU.subtract).then_inc(k_lo, 1)

            def setup_w2():
                dve.wait_ge(k_mean_sb, 2)
                for m in range(2):
                    for c in range(CB):
                        last = nc.vector.scalar_tensor_tensor(
                            piece(1 + m)[:, c, :], piece(1 + m)[:, c, :], gamma_sb[:, m * CB + c:m * CB + c + 1],
                            z[:, :], ALU.mult, ALU.subtract)
                    last.then_inc(k_cent, 1)
                dve.wait_ge(k_cent, 2)
                rest_of(1)
                rest_of(2)

            def setup_w1():
                rest_of(3)
                rest_of(4)

            rest_of(0)

            def turn(t):
                g = t.plus(1)
                if g.within(NG):
                    for b in range(2):
                        half = att[:, b * HH:(b + 1) * HH, :].rearrange("p h n -> p (h n)")
                        dve.wait_ge(s_sloped, g.count(per=2) - 1 + b)
                        nc.vector.tensor_tensor(half, p_att[:, b * HALF:(b + 1) * HALF], half, ALU.max).then_inc(s_leaky, 1)
                    for b in range(2):
                        half = att[:, b * HH:(b + 1) * HH, :]
                        dve.wait_ge(s_leaky, g.count(per=2) - 1 + b)
                        if b == 0:
                            dve.wait_ge(s_mask, g.count())
                        nc.vector.tensor_tensor(half, half, mask[:, :].unsqueeze(1).broadcast_to([P, HH, N]),
                                                ALU.add).then_inc(s_masked, 1)
                    for b in range(2):
                        dve.wait_ge(s_masked, g.count(per=2) - 1 + b)
                        nc.vector.reduce_max(neg_max[:, b * HH:(b + 1) * HH], att[:, b * HH:(b + 1) * HH, :], X,
                                             negate=True).then_inc(s_max, 1)
                g = t
                if g.within(NG):
                    dve.wait_ge(s_w1, g.count(per=2) - 1)
                    dve.wait_ge(s_inv, g.plus(1).count())
                    if g.has(1):
                        dve.wait_ge(s_rT, g.count(1, per=2))
                    nc.vector.scalar_tensor_tensor(r[:, 0:HALF], p_w1a[:, :], inv[:, g.slot(4), 0:1],
                                                   b1_bc[:, 0:HALF], ALU.mult, ALU.add).then_inc(s_pre, 1)
                g = t.plus(2)
                if g.within(NG):
                    dve.wait_ge(s_h0_hi, g.count())
                    nc.vector.scalar_tensor_tensor(h0[:, :, 1, :], p_ta[:, :].rearrange("p (c n) -> p c n", n=N), 0.0, h0[:, :, 0, :],
                                                   ALU.max, ALU.subtract).then_inc(s_h0_lo, 1)
                    dve.wait_ge(s_in[g.slot(4)], g.uses(4, 32))
                    if g.has(2):
                        dve.wait_ge(s_G, g.count(2))
                        dve.wait_ge(s_beT, g.count(2))
                    nc.vector.tensor_scalar(inc[:, g.slot(2), :, :], adj_in[:, g.slot(4), :, :], 0.0, None,
                                            ALU.not_equal).then_inc(s_inc, 1)
                    dve.wait_ge(s_inc, g.count())
                    nc.vector.reduce_sum(G[:, g.plus(-1).slot(4), N + 1:N + 2], inc[:, g.slot(2), 1, :], X).then_inc(s_sizes, 1)
                g = t.plus(-1)
                if g.within(NG):
                    dve.wait_ge(s_y, g.count())
                    dve.wait_ge(s_rest, g.count())
                    if g.has(2):
                        dve.wait_ge(s_out[g.slot(2)], g.plus(-2).uses(2, 16))
                    nc.vector.scalar_tensor_tensor(y[:, g.slot(2), :], p_tb[:, :], inv[:, g.slot(4), 0:1],
                                                   rest[:, g.slot(2), :], ALU.mult, ALU.add).then_inc(s_y_sb, 1)
                g = t
                if g.within(NG):
                    dve.wait_ge(s_r, g.count(per=2) - 1)
                    nc.vector.bn_stats(st2[:, 0, :], r[:, 0:HALF]).then_inc(s_stats2, 1)
                g = t.plus(3)
                if g.within(NG):
                    dve.wait_ge(s_in[g.slot(4)], g.uses(4, 32))
                    nc.vector.bn_stats(st0[:, :], x_in[:, g.slot(4), :]).then_inc(s_stats0, 1)
                    dve.wait_ge(s_stats0, g.count())
                g = t
                if g.within(NG):
                    dve.wait_ge(s_w1, g.count(per=2))
                    nc.vector.scalar_tensor_tensor(r[:, HALF:DH], p_w1b[:, :], inv[:, g.slot(4), 0:1],
                                                   b1_bc[:, HALF:DH], ALU.mult, ALU.add).then_inc(s_pre, 1)
                g = t.plus(3)
                if g.within(NG):
                    nc.vector.bn_aggr(mv0[:, :], st0[:, :]).then_inc(s_mv0, 1)
                g = t
                if g.within(NG):
                    dve.wait_ge(s_rT_hi, g.count(per=2) - 1)
                    nc.vector.tensor_tensor(rT_lo[:, 0:HALF], p_ta[:, :], rT_hi[:, 0:HALF],
                                            ALU.subtract).then_inc(s_rT_lo, 1)
                    dve.wait_ge(s_r, g.count(per=2))
                    nc.vector.bn_stats(st2[:, 1, :], r[:, HALF:DH]).then_inc(s_stats2, 1)
                    dve.wait_ge(s_stats2, g.count(per=2))
                g = t.plus(2)
                if g.within(NG):
                    dve.wait_ge(s_e_hi, g.count())
                    nc.vector.tensor_tensor(e_rest[:, :], p_e[0:64, N:2 * N], e_hi[:, :], ALU.subtract).then_inc(s_e_rest, 1)
                if t.within(NG):
                    nc.vector.bn_aggr(mv2[:, :], st2[:, :, :].rearrange("p a b -> p (a b)")).then_inc(s_mv2, 1)
                if g.within(NG):
                    dve.wait_ge(s_e_rest, g.count())
                    if g.has(1):
                        dve.wait_ge(s_en_rhs, g.count(1))
                    nc.vector.scalar_tensor_tensor(en_parts[32:64, :], e_rest[32:64, :], lo_rows[32:64, :], p_e[32:64, 0:N],
                                                   ALU.mult, ALU.add).then_inc(s_en_parts, 1)
                    if g.has(1):
                        dve.wait_ge(s_scores, g.count(1, per=2))
                    nc.vector.scalar_tensor_tensor(es_lhs[0:32, :], e_rest[0:32, :], lo_rows[0:32, :], p_e[0:32, 0:N],
                                                   ALU.mult, ALU.add).then_inc(s_es_lhs, 1)
                if g.within(NG + 1):
                    if g.within(NG):
                        dve.wait_ge(s_sizes, g.count())
                    if g.has(1):
                        dve.wait_ge(s_G_sb, g.count(1))
                    nc.vector.tensor_scalar(cnt[:, :], G[:, g.plus(-1).slot(4), N:N + 2], TINY, None, ALU.max).then_inc(s_cnt1, 1)
                    dve.wait_ge(s_cnt1, g.count())
                    nc.vector.reciprocal(inv0[:, :], cnt[:, :]).then_inc(s_inv0, 1)
                g = t.plus(1)
                if g.within(NG):
                    s = g.slot(2)
                    dve.wait_ge(s_o, g.count())
                    nc.vector.reciprocal(rden[:, :].rearrange("p (b h) -> p b h", b=2), p_o[:, :, :, UN]).then_inc(s_rden, 1)
                    dve.wait_ge(s_rden, g.count())
                    nc.vector.tensor_tensor(o_sc[:, :].rearrange("p (b h u) -> p b h u", b=2, u=UN),
                                            p_o[:, :, :, 0:UN],
                                            rden[:, :].rearrange("p (b h) -> p b h", b=2).unsqueeze(3).broadcast_to([P, 2, HH, UN]),
                                            ALU.mult).then_inc(s_osc, 1)
                if g.within(NG):
                    dve.wait_ge(s_osc, g.count())
                    if g.has(2):
                        dve.wait_ge(s_xh, g.count(2))
                    nc.vector.scalar_tensor_tensor(x1[:, s, :], o_sc[:, :], 0.0, x_in[:, g.slot(4), :],
                                                   ALU.max, ALU.add).then_inc(s_x1, 1)
                if t.within(NG):
                    dve.wait_ge(s_rT_hi, t.count(per=2))
                    nc.vector.tensor_tensor(rT_lo[:, HALF:DH], p_tb[:, :], rT_hi[:, HALF:DH],
                                            ALU.subtract).then_inc(s_rT_lo, 1)
                if g.within(NG):
                    dve.wait_ge(s_x1, g.count())
                    nc.vector.bn_stats(st1[:, :], x1[:, s, :]).then_inc(s_stats1, 1)
                    dve.wait_ge(s_stats1, g.count())
                g = t.plus(2)
                if g.within(NG + 1):
                    dve.wait_ge(s_inv0, g.count())
                    if g.has(4):
                        dve.wait_ge(s_beT, g.count(4))
                    nc.vector.scalar_tensor_tensor(inv[:, g.plus(-1).slot(4), :], G[:, g.plus(-1).slot(4), N:N + 2], 0.0, inv0[:, :],
                                                   ALU.is_gt, ALU.mult).then_inc(s_inv, 1)
                g = t.plus(1)
                if g.within(NG):
                    nc.vector.bn_aggr(mv1[:, :], st1[:, :]).then_inc(s_mv1, 1)
                g = t.plus(2)
                if g.within(NG):
                    dve.wait_ge(s_feats, g.count())
                    if g.has(2):
                        dve.wait_ge(s_o, g.count(2))
                    nc.vector.tensor_tensor(feats[:, g.slot(2), :, 0:UN],
                                            p_f[:, :].rearrange("p (h u) -> p h u", u=UN),
                                            b0_bc[:, :].rearrange("p (h u) -> p h u", u=UN),
                                            ALU.add).then_inc(s_feats_sb, 1)
                g = t
                if g.within(NG):
                    dve.wait_ge(s_w2, g.count())
                    dve.wait_ge(s_rs2, g.count())
                    if g.has(1):
                        dve.wait_ge(s_y, g.count(1))
                    nc.vector.scalar_tensor_tensor(z[:, :], p_w1a[:, :], rs2[:, :], t_bc[:, :],
                                                   ALU.mult, ALU.add).then_inc(s_z, 1)
                g = t.plus(1)
                if g.within(NG):
                    dve.wait_ge(s_hg_hi, g.count())
                    nc.vector.tensor_tensor(hg_lo[:, :], p_w1b[:, :], hg_hi[:, :], ALU.subtract).then_inc(s_hg_lo, 1)

            turns(dve, turn, NG, {-1: setup_w2, 0: setup_w1})

        @block.tensor
        def _(pe):
            mm = nc.tensor.matmul
            pe.wait_ge(k_const, 3)
            pe.wait_ge(k_wa, 6)
            pe.wait_ge(k_lo, 1)

            def setup_w2():
                pe.wait_ge(s_stage[1], 16)
                pe.wait_ge(s_stage[0], 32)
                for vec, dst, s in ((gamma_sb, p_w1a, k_mean), (beta_sb, p_w1b, k_t)):
                    for c in range(HC):
                        last = mm(dst[:, :], vec[:, c:c + 1].broadcast_to([P, P]), piece(1 + c // CB)[:, c % CB, :],
                                  start=c == 0, stop=c == HC - 1)
                    last.then_inc(s, 1)

            def setup_done():
                pe.wait_ge(k_lo, len(PIECES))
                pe.wait_ge(k_mean_sb, 2)

            def three(dst, hi, lo, w_hi, w_lo, first, final):
                mm(dst, hi, w_hi, start=first, stop=False)
                mm(dst, hi, w_lo, start=False, stop=False)
                return mm(dst, lo, w_hi, start=False, stop=final)

            def hidden(g, half, dst):
                for c in range(DC):
                    k = slice(c * P, (c + 1) * P)
                    n = slice(half * HALF, (half + 1) * HALF)
                    last = three(dst[:, :], hg_hi[:, k], hg_lo[:, k], W1_hi[:, c, n], W1_lo[:, c, n], c == 0, c == DC - 1)
                last.then_inc(s_w1, 1)

            def transposes(dst, src, s):
                for c in range(HALF // P):
                    last = nc.tensor.transpose(dst[:, c * P:(c + 1) * P], src[:, c * P:(c + 1) * P], ident[:, :])
                last.then_inc(s, 1)

            def turn(t):
                g = t
                if g.within(NG):
                    pe.wait_ge(s_hg_lo, g.count())
                    if g.has(1):
                        pe.wait_ge(s_z, g.count(1))
                    hidden(g, 0, p_w1a)
                    hidden(g, 1, p_w1b)
                g = t
                if g.within(NG):
                    pe.wait_ge(s_r, g.count(per=2) - 1)
                    if g.plus(2).within(NG):
                        pe.wait_ge(s_h0_lo, g.plus(2).count())
                    transposes(p_ta, r[:, 0:HALF], s_rT)
                g = t.plus(2)
                if g.within(NG):
                    pe.wait_ge(s_h0_lo, g.count())
                    if g.has(1):
                        pe.wait_ge(s_feats_sb, g.count(1))
                        pe.wait_ge(s_es_lhs, g.count(1))
                        pe.wait_ge(s_G_sb, g.count(1))
                    for c in range(DC):
                        last = mm(p_e, Wa[:, c, :], h0[:, c, :, :].rearrange("p a n -> p (a n)"), start=c == 0, stop=c == DC - 1)
                    last.then_inc(s_e, 1)
                g = t.plus(1)
                if g.within(NG):
                    pe.wait_ge(s_exp, g.count(per=2))
                    for i in range(HEADS):
                        last = nc.tensor.transpose(p_att[:, i * N:(i + 1) * N], att[:, i, :], ident[:, :])
                    last.then_inc(s_attT, 1)
                g = t.plus(2)
                if g.within(NG):
                    for c in range(DC):
                        last = three(p_f[:, :], h0[:, c, 0, :], h0[:, c, 1, :], W0_hi[:, c, :], W0_lo[:, c, :], c == 0, c == DC - 1)
                    last.then_inc(s_feats, 1)
                g = t.plus(1)
                if g.within(NG):
                    pe.wait_ge(s_attT_sb, g.count())
                    pe.wait_ge(s_feats_sb, g.count())
                    for i in range(HEADS):
                        last = mm(p_o[:, i // HH, i % HH, :], attT[:, i, :], feats[:, g.slot(2), i, :], start=True, stop=True)
                    last.then_inc(s_o, 1)
                g = t
                if g.within(NG):
                    pe.wait_ge(s_r, g.count(per=2))
                    if g.has(1):
                        pe.wait_ge(s_y_sb, g.count(1))
                    transposes(p_tb, r[:, HALF:DH], s_rT)
                g = t
                if g.within(NG):
                    for c in range(HC):
                        if c % CB == 0:
                            pe.wait_ge(s_rT_lo, g.count(per=2) - 1 + c // CB)
                        k = slice(c * P, (c + 1) * P)
                        last = three(p_w1a[:, :], rT_hi[:, k], rT_lo[:, k], W2_hi[:, c, :], W2_lo[:, c, :], c == 0, c == HC - 1)
                    last.then_inc(s_w2, 1)
                g = t.plus(1)
                if g.within(NG):
                    pe.wait_ge(s_h, g.count())
                    pe.wait_ge(s_G_sb, g.count())
                    if g.has(1):
                        pe.wait_ge(s_pre, g.count(1, per=2))
                    for c in range(DC):
                        last = mm(p_w1b[:, c * P:(c + 1) * P], h[:, g.slot(2), c * P:(c + 1) * P], G[:, g.slot(4), 0:N],
                                  start=True, stop=True)
                    last.then_inc(s_hg, 1)
                g = t.plus(2)
                if g.within(NG):
                    pe.wait_ge(s_en_rhs, g.count())
                    pe.wait_ge(s_es_lhs, g.count())
                    if g.has(1):
                        pe.wait_ge(s_osc, g.count(1))
                    for b in range(2):
                        dst = p_att[:, b * HALF:(b + 1) * HALF]
                        last = mm(dst, es_lhs[:, :], en_rhs[:, b * HH:(b + 1) * HH, :].rearrange("p h n -> p (h n)"),
                                  start=True, stop=True)
                        last.then_inc(s_scores, 1)
                    pe.wait_ge(s_beT, g.count())
                    pe.wait_ge(s_row, g.count())
                    if g.has(1):
                        pe.wait_ge(s_G_sb, g.count(1))
                    mm(p_G, inc[:, g.slot(2), 1, :], beT[:, :], start=True, stop=True).then_inc(s_G, 1)
                g = t.plus(3)
                if g.within(NG):
                    pe.wait_ge(s_xn, g.count())
                    if t.within(NG):
                        pe.wait_ge(s_rT_lo, t.count(per=2) - 1)
                    elif g.has(1):
                        pe.wait_ge(s_h0_lo, g.count(1))
                    transposes(p_ta, xn, s_xnT)
                g = t
                if g.within(NG):
                    pe.wait_ge(s_z, g.count())
                    pe.wait_ge(s_rT_lo, g.count(per=2))
                    mm(p_tb[:, :], G[:, g.slot(4), 0:N], z[:, :], start=True, stop=True).then_inc(s_y, 1)

            turns(pe, turn, NG, {-2: setup_w2, 0: setup_done})


_INS = ["x", "adj2", "W0T", "b0", "a_self", "a_neigh", "W1T", "b1", "gammaT", "betaT", "W2T", "b2"]


def kernel(x, adj, L0_gnn_W, L0_gnn_b, L0_gnn_a_self, L0_gnn_a_neigh, L1_gnn_W1, L1_gnn_b1, L1_gnn_gamma,
           L1_gnn_beta, L1_gnn_W2, L1_gnn_b2):
    import numpy as np
    import concourse.bacc as bacc
    from concourse.bass_utils import run_bass_kernel_spmd

    adj = np.asarray(adj)
    f = np.asarray(L0_gnn_W).shape[1]
    laid = {
        "x": x,
        "adj2": np.stack([adj, adj.transpose(0, 2, 1)], axis=2),
        "W0T": np.asarray(L0_gnn_W).transpose(1, 0, 2).reshape(f, -1),
        "b0": L0_gnn_b, "a_self": L0_gnn_a_self, "a_neigh": L0_gnn_a_neigh,
        "W1T": np.asarray(L1_gnn_W1).T, "b1": L1_gnn_b1,
        "gammaT": np.asarray(L1_gnn_gamma).reshape(-1, P).T, "betaT": np.asarray(L1_gnn_beta).reshape(-1, P).T,
        "W2T": np.asarray(L1_gnn_W2).T, "b2": L1_gnn_b2,
    }
    nc = bacc.Bacc("TRN2", target_bir_lowering=False, num_devices=1)
    arrays, args = {}, []
    for name in _INS:
        a = np.ascontiguousarray(laid[name])
        arrays[f"in_{name}"] = a
        args.append(nc.dram_tensor(f"in_{name}", a.shape, mybir.dt.from_np(a.dtype), kind="ExternalInput").ap())
    out = nc.dram_tensor("out", arrays["in_x"].shape, F32, kind="ExternalOutput").ap()
    gnn_two_layers(nc, *args, out)
    got = run_bass_kernel_spmd(nc, [arrays], core_ids=[0])
    return got.results[0]["out"]
```

```python
import concourse.bass as bass
from concourse import mybir
from contextlib import ExitStack

F32 = mybir.dt.float32
F32R = mybir.dt.float32r
ALU = mybir.AluOpType
ACT = mybir.ActivationFunctionType
X = mybir.AxisListType.X

P = 128
AHEAD = 3
UNROLL = 4
EPS = 1e-5
SLOPE = 0.2
NEG_BIG = -1e10
TINY = 1e-30


class Graph:

    def __init__(self, base, loop=None):
        self.base, self.loop = base, loop

    def plus(self, n):
        return Graph(self.base + n, self.loop)

    def within(self, total):
        return self.loop is not None or 0 <= self.base < total

    def slot(self, ring):
        return self.base % ring

    def has(self, back):
        return self.loop is not None or self.base >= back

    def count(self, back=0, per=1):
        n = (self.base + 1 - back) * per
        return n if self.loop is None else self.loop * (UNROLL * per) + n

    def uses(self, ring, per):
        n = (self.base // ring + 1) * per
        return n if self.loop is None else self.loop * (UNROLL // ring * per) + n


def turns(eng, turn, total, before={}):
    loops = (total - AHEAD - 2) // UNROLL
    for t in range(-AHEAD, 1):
        if t in before:
            before[t]()
        turn(Graph(t))
    with eng.Fori(0, loops) as k:
        for u in range(1, UNROLL + 1):
            turn(Graph(u, k))
    for t in range(1 + loops * UNROLL, total + 1):
        turn(Graph(t))


def gnn_two_layers(nc, x, adj2, W0T, b0, a_self, a_neigh, W1T, b1, gammaT, betaT, W2T, b2, out):
    NG, N, D = x.shape
    HEADS = a_self.shape[0]
    UN = D // HEADS
    DH = W1T.shape[1]
    DC, HC = D // P, DH // P
    HALF = 512
    HH = HEADS // 2
    CB = HC // 2
    UE = UN + 1
    HN = HEADS * N

    ctx = ExitStack()
    with ctx:
        def sb(name, shape, dt=F32):
            return ctx.enter_context(nc.sbuf_tensor(name, shape, dt))

        def sem(name):
            return ctx.enter_context(nc.semaphore(name))

        W0_hi, W0_lo = (sb(n, [P, DC, D], F32R) for n in ("W0_hi", "W0_lo"))
        Wa = sb("Wa", [P, DC, P], F32R)
        W1_hi, W1_lo = (sb(n, [P, DC, DH], F32R) for n in ("W1_hi", "W1_lo"))
        W2_hi, W2_lo = (sb(n, [P, HC, D], F32R) for n in ("W2_hi", "W2_lo"))
        raw = sb("raw", [P, 4, 4 * HALF])
        ident = sb("ident", [P, P])
        ones = sb("ones", [P, P])
        halfpow = sb("halfpow", [P, 1])
        eps = sb("eps", [P, 1])
        neg_one = sb("neg_one", [P, 1])
        neg_big = sb("neg_big", [P, 1])
        b0_bc = sb("b0_bc", [P, D])
        b1_bc = sb("b1_bc", [P, DH])
        b2_bc = sb("b2_bc", [P, D])
        t_bc = sb("t_bc", [P, D])
        gamma_beta = sb("gamma_beta", [P, 2, HC])
        head_rows = sb("head_rows", [64, HEADS])
        lo_rows8 = sb("lo_rows8", [64, HEADS])
        lo_rows = sb("lo_rows", [64, 1])
        x_in = sb("x_in", [P, 4, D])
        adj_in = sb("adj_in", [P, 4, 2, N])
        inc = sb("inc", [P, 2, 2, N])
        mask = sb("mask", [P, N])
        cnt = sb("cnt", [P, 2])
        inv0 = sb("inv0", [P, 2])
        inv = sb("inv", [P, 4, 2])
        beT = sb("beT", [P, N + 1])
        G = sb("G", [P, 4, N + 2])
        G_hi, G_lo = sb("G_hi", [P, N], F32R), sb("G_lo", [P, N], F32R)
        st0 = sb("st0", [P, 6])
        st1 = sb("st1", [P, 6])
        st2 = sb("st2", [P, 2, 6])
        mv0 = sb("mv0", [P, 2])
        mv1 = sb("mv1", [P, 2])
        mv2 = sb("mv2", [P, 2])
        ve0, ve1, ve2 = sb("ve0", [P, 1]), sb("ve1", [P, 1]), sb("ve2", [P, 1])
        rs0, rs1, rs2 = sb("rs0", [P, 1]), sb("rs1", [P, 1]), sb("rs2", [P, 1])
        nm0, nm1 = sb("nm0", [P, 1]), sb("nm1", [P, 1])
        nb0, nb1 = sb("nb0", [P, 1]), sb("nb1", [P, 1])
        xn = sb("xn", [P, D])
        h0 = sb("h0", [P, DC, 2, N], F32R)
        feats = sb("feats", [P, 2, HEADS, UE])
        e_hi = sb("e_hi", [64, N], F32R)
        e_rest = sb("e_rest", [64, N])
        en_parts = sb("en_parts", [64, N])
        es_lhs = sb("es_lhs", [64, N], F32R)
        en_rhs = sb("en_rhs", [64, HEADS, N], F32R)
        att = sb("att", [P, HEADS, N])
        neg_max = sb("neg_max", [P, HEADS])
        attT = sb("attT", [P, HEADS, N])
        rden = sb("rden", [P, HEADS])
        o_sc = sb("o_sc", [P, D])
        x1 = sb("x1", [P, 2, D])
        h = sb("h", [P, 2, D])
        rest = sb("rest", [P, 2, D])
        hg_hi, hg_lo = sb("hg_hi", [P, D], F32R), sb("hg_lo", [P, D], F32R)
        r = sb("r", [P, DH])
        rT_hi, rT_lo = sb("rT_hi", [P, DH], F32R), sb("rT_lo", [P, DH], F32R)
        z = sb("z", [P, D])
        z_hi, z_lo = sb("z_hi", [P, D], F32R), sb("z_lo", [P, D], F32R)
        y = raw[:, 1, 0:2 * D].rearrange("p (s n) -> p s n", s=2)

        def bank(name, n=1):
            return ctx.enter_context(nc.psum_tensor(name, [P, n * HALF], F32))

        p_w1a = bank("p_w1a")
        p_w1b = bank("p_w1b")
        p_att = bank("p_att", 2)
        p_ta = bank("p_ta")
        p_tb = bank("p_tb")
        p_f = bank("p_f")
        p_s = bank("p_s")
        p_e = p_s[:, 0:2 * N]
        p_G = p_s[:, 2 * N:3 * N + 1]
        p_o = p_att[:, :].rearrange("p (b c) -> p b c", b=2)[:, :, 0:HH * UE].rearrange("p b (h u) -> p b h u", u=UE)

        s_in = [sem(f"s_in{i}") for i in range(4)]
        s_out = [sem(f"s_out{i}") for i in range(2)]
        s_vectors, s_small = sem("s_vectors"), sem("s_small")
        s_raw = [sem(f"s_raw{i}") for i in range(5)]
        k_ones, k_ident, k_rows, k_lorow = sem("k_ones"), sem("k_ident"), sem("k_rows"), sem("k_lorow")
        k_prod_self, k_prod_neigh, k_pulled, k_wa0, k_wa = (sem("k_" + n) for n in ("prod_self", "prod_neigh", "pulled", "wa0", "wa"))
        k_hi, k_lo0, k_lo1, k_lo2 = sem("k_hi"), sem("k_lo0"), sem("k_lo1"), sem("k_lo2")
        k_sums, k_sums_sb, k_mean, k_mean_sb, k_cent = sem("k_sums"), sem("k_sums_sb"), sem("k_mean"), sem("k_mean_sb"), sem("k_cent")
        s_stats0, s_mv0, s_ve0, s_rs0, s_nm0, s_nb0, s_xn, s_xnT = (sem("s_" + n) for n in ("stats0", "mv0", "ve0", "rs0", "nm0", "nb0", "xn", "xnT"))
        s_h0_hi, s_h0_lo, s_feats, s_feats_sb = (sem("s_" + n) for n in ("h0_hi", "h0_lo", "feats", "feats_sb"))
        s_e_hi, s_e_rest, s_es_lhs, s_en_parts, s_en_rhs = (sem("s_" + n) for n in ("e_hi", "e_rest", "es_lhs", "en_parts", "en_rhs"))
        s_absent, s_mask, s_scores, s_sloped, s_leaky, s_masked, s_max = (sem("s_" + n) for n in ("absent", "mask", "scores", "sloped", "leaky", "masked", "max"))
        s_exp, s_attT, s_attT_sb, s_o, s_rden, s_osc, s_x1 = (sem("s_" + n) for n in ("exp", "attT", "attT_sb", "o", "rden", "osc", "x1"))
        s_inc, s_sizes, s_e, s_row, s_cnt1, s_inv0, s_inv, s_beT, s_G, s_G_sb = (sem("s_" + n) for n in ("inc", "sizes", "e", "row", "cnt1", "inv0", "inv", "beT", "G", "G_sb"))
        s_stats1, s_mv1, s_ve1, s_rs1, s_nm1, s_nb1, s_h, s_xh, s_rest = (sem("s_" + n) for n in ("stats1", "mv1", "ve1", "rs1", "nm1", "nb1", "h", "xh", "rest"))
        s_hg, s_hg_hi, s_hg_lo, s_w1, s_pre, s_r = (sem("s_" + n) for n in ("hg", "hg_hi", "hg_lo", "w1", "pre", "r"))
        s_stats2, s_mv2, s_ve2, s_rs2, s_rT, s_rT_hi, s_rT_lo = (sem("s_" + n) for n in ("stats2", "mv2", "ve2", "rs2", "rT", "rT_hi", "rT_lo"))
        s_w2, s_z, s_z_hi, s_z_lo, s_y, s_y_sb = (sem("s_" + n) for n in ("w2", "z", "z_hi", "z_lo", "y", "y_sb"))
        s_G_hi, s_G_lo = sem("s_G_hi"), sem("s_G_lo")

        block = ctx.enter_context(nc.Block())

        W0v, W1v, W2v = (w.rearrange("(c p) n -> p c n", p=P) for w in (W0T, W1T, W2T))
        PIECES = [
            (W0v, W0_hi[:, :, :], W0_lo[:, :, :]),
            (W1v[:, :, 0:HALF], W1_hi[:, :, 0:HALF], W1_lo[:, :, 0:HALF]),
            (W1v[:, :, HALF:DH], W1_hi[:, :, HALF:DH], W1_lo[:, :, HALF:DH]),
            (W2v[:, 0:CB, :], W2_hi[:, 0:CB, :], W2_lo[:, 0:CB, :]),
            (W2v[:, CB:HC, :], W2_hi[:, CB:HC, :], W2_lo[:, CB:HC, :]),
        ]

        def piece(n):
            return raw[:, n % 4, :].rearrange("p (c n) -> p c n", c=4)

        SMALL = 5
        a_bc = h
        wa_raw = r[:, 0:2 * DC * HEADS].rearrange("p (a c n) -> p a c n", a=2, c=DC)
        prod_self = att[:, :, :].rearrange("p h n -> p (h n)")
        prod_neigh = [attT[:, :, :].rearrange("p h n -> p (h n)")[:, 0:D], attT[:, :, :].rearrange("p h n -> p (h n)")[:, D:2 * D],
                      rest[:, 0, :], rest[:, 1, :]]
        sums_sb, mean_sb = z, raw[:, 2, 0:D]

        @block.sync
        def _(sp):
            def load(g):
                if g.has(4):
                    sp.wait_ge(s_x1, g.count(4))
                    sp.wait_ge(s_inc, g.count(4))
                    sp.wait_ge(s_mask, g.count(4))
                    sp.wait_ge(s_row, g.count(4))
                s = g.slot(4)
                n = g.base if g.loop is None else g.loop * UNROLL + g.base
                sp.dma_start(x_in[:, s, :], x[bass.ds(n, 1), :, :].rearrange("a p d -> p (a d)")).then_inc(s_in[s], 16)
                sp.dma_start(adj_in[:, s, :, :], adj2[bass.ds(n, 1), :, :, :].rearrange("a p t n -> p (a t) n")).then_inc(s_in[s], 16)

            def load_piece(n):
                if n == 4:
                    sp.wait_ge(k_prod_self, DC)
                    sp.wait_ge(k_prod_neigh, DC)
                    sp.wait_ge(k_lo0, 1)
                sp.dma_start(piece(n), PIECES[n][0]).then_inc(s_raw[n], 16)

            def bc(v, n):
                return v.rearrange("(a n) -> a n", a=1).broadcast_to([P, n])

            load(Graph(0))
            load_piece(0)
            sp.dma_start(a_bc[:, 0, :], bc(a_self.rearrange("h u -> (h u)"), D)).then_inc(s_vectors, 16)
            sp.dma_start(a_bc[:, 1, :], bc(a_neigh.rearrange("h u -> (h u)"), D)).then_inc(s_vectors, 16)
            load_piece(1)
            load(Graph(1))
            sp.dma_start(gamma_beta[:, 0, :], gammaT).then_inc(s_small, 16)
            sp.dma_start(gamma_beta[:, 1, :], betaT).then_inc(s_small, 16)
            sp.dma_start(b0_bc[:, :], bc(b0.rearrange("h u -> (h u)"), D)).then_inc(s_small, 16)
            sp.dma_start(b1_bc[:, :], bc(b1, DH)).then_inc(s_small, 16)
            sp.dma_start(b2_bc[:, :], bc(b2, D)).then_inc(s_small, 16)
            load_piece(2)
            load_piece(3)
            load(Graph(2))
            load_piece(4)
            load(Graph(3))

            def turn(t):
                g = t.plus(-1)
                if g.within(NG):
                    sp.wait_ge(s_y_sb, g.count())
                    n = g.base if g.loop is None else g.loop * UNROLL + g.base
                    sp.dma_start(out[bass.ds(n, 1), :, :].rearrange("a p d -> p (a d)"), y[:, g.slot(2), :]).then_inc(s_out[g.slot(2)], 16)
                g = t.plus(4)
                if g.within(NG) and (g.loop is not None or g.base >= 4):
                    load(g)

            turns(sp, turn, NG)
            for i in range(2):
                sp.wait_ge(s_out[i], 16 * (NG // 2))

        @block.gpsimd
        def _(pool):
            nc.gpsimd.memset(ident[:, :], 0.0).then_inc(k_ones, 1)
            nc.gpsimd.memset(ones[:, :], 1.0).then_inc(k_ones, 1)
            nc.gpsimd.memset(head_rows[:, :], 0.0).then_inc(k_ones, 1)
            nc.gpsimd.memset(lo_rows8[:, :], 0.0).then_inc(k_ones, 1)
            nc.gpsimd.memset(halfpow[:, :], -0.5).then_inc(k_ones, 1)
            nc.gpsimd.memset(eps[:, :], EPS).then_inc(k_ones, 1)
            nc.gpsimd.memset(neg_one[:, :], -1.0).then_inc(k_ones, 1)
            nc.gpsimd.memset(neg_big[:, :], NEG_BIG).then_inc(k_ones, 1)
            nc.gpsimd.memset(G[:, 3, N:N + 2], 1.0).then_inc(k_ones, 1)
            nc.gpsimd.memset(feats[:, :, :, UN:UE], 1.0).then_inc(k_ones, 1)
            pool.wait_ge(k_ones, 10)
            nc.gpsimd.affine_select(out=ident[:, :], in_=ident[:, :], compare_op=ALU.not_equal, fill=1.0,
                                    base=0, pattern=[[-1, P]], channel_multiplier=1).then_inc(k_ident, 1)
            done = 10
            for first in (0, HEADS, 2 * HEADS, 32, 32 + HEADS, 32 + 2 * HEADS):
                for rows in (head_rows, lo_rows8):
                    if rows is head_rows or first in (HEADS, 32 + HEADS):
                        pool.wait_ge(k_ones, done)
                        nc.gpsimd.affine_select(out=rows[:, :], in_=rows[:, :], compare_op=ALU.not_equal,
                                                fill=1.0, base=-first, pattern=[[-1, HEADS]],
                                                channel_multiplier=1).then_inc(k_ones, 1)
                        done += 1
            pool.wait_ge(k_ones, done)

            def split_rest(n, his, lo):
                pool.wait_ge(k_hi, his)
                nc.gpsimd.tensor_tensor(PIECES[n][2], piece(n), PIECES[n][1], ALU.subtract).then_inc(lo, 1)

            def setup_w0():
                pool.wait_ge(s_raw[0], 16)
                pool.wait_ge(s_vectors, 32)
                for c in range(DC):
                    nc.gpsimd.tensor_tensor(prod_neigh[c], piece(0)[:, c, :], a_bc[:, 1, :], ALU.mult).then_inc(k_prod_neigh, 1)
                split_rest(0, 1, k_lo0)

            def setup_w2():
                for n in (3, 4):
                    split_rest(n, n + 1, k_lo2)

            def rstd(g, mv, ve, rs, s_mv, s_ve, s_rs, s_free, nm=None, s_nm=None):
                pool.wait_ge(s_mv, g.count())
                nc.gpsimd.tensor_tensor(ve[:, :], mv[:, 1:2], eps[:, :], ALU.add).then_inc(s_ve, 1)
                if g.has(1):
                    pool.wait_ge(s_free, g.count(1))
                if nm is not None:
                    nc.gpsimd.tensor_tensor(nm[:, :], mv[:, 0:1], neg_one[:, :], ALU.mult).then_inc(s_nm, 1)
                pool.wait_ge(s_ve, g.count())
                nc.gpsimd.tensor_tensor(rs[:, :], ve[:, :], halfpow[:, :], ALU.pow).then_inc(s_rs, 1)

            def shift(g, nm, rs, nb, s_nm, s_rs, s_nb):
                pool.wait_ge(s_nm, g.count())
                pool.wait_ge(s_rs, g.count())
                nc.gpsimd.tensor_tensor(nb[:, :], nm[:, :], rs[:, :], ALU.mult).then_inc(s_nb, 1)

            def turn(t):
                g = t.plus(2)
                if g.within(NG):
                    pool.wait_ge(s_in[g.slot(4)], g.uses(4, 32))
                    if g.has(1):
                        pool.wait_ge(s_masked, g.count(1, per=2))
                    nc.gpsimd.tensor_tensor(mask[:, :], ones[:, :], adj_in[:, g.slot(4), 0, :], ALU.subtract).then_inc(s_absent, 1)
                    pool.wait_ge(s_absent, g.count())
                    nc.gpsimd.tensor_tensor(mask[:, :], mask[:, :], neg_big[:, :].broadcast_to([P, N]), ALU.mult).then_inc(s_mask, 1)
                g = t.plus(3)
                if g.within(NG):
                    rstd(g, mv0, ve0, rs0, s_mv0, s_ve0, s_rs0, s_xn, nm0, s_nm0)
                    shift(g, nm0, rs0, nb0, s_nm0, s_rs0, s_nb0)
                g = t
                if g.within(NG):
                    rstd(g, mv2, ve2, rs2, s_mv2, s_ve2, s_rs2, s_z)
                g = t.plus(2)
                if g.within(NG):
                    pool.wait_ge(s_en_parts, g.count())
                    pool.wait_ge(s_mask, g.count())
                    if g.plus(1).within(NG):
                        pool.wait_ge(s_nb0, g.plus(1).count())
                    if t.within(NG):
                        pool.wait_ge(s_rs2, t.count())
                    if g.has(1):
                        pool.wait_ge(s_scores, g.count(1, per=2))
                    nc.gpsimd.tensor_tensor(en_rhs[32:64, :, :],
                                            en_parts[32:64, :].unsqueeze(1).broadcast_to([32, HEADS, N]),
                                            head_rows[32:64, :].unsqueeze(2).broadcast_to([32, HEADS, N]), ALU.mult).then_inc(s_en_rhs, 1)
                g = t.plus(1)
                if g.within(NG):
                    if g.plus(1).within(NG):
                        pool.wait_ge(s_en_rhs, g.plus(1).count())
                    rstd(g, mv1, ve1, rs1, s_mv1, s_ve1, s_rs1, s_h, nm1, s_nm1)
                    shift(g, nm1, rs1, nb1, s_nm1, s_rs1, s_nb1)
                g = t.plus(2)
                if g.within(NG):
                    pool.wait_ge(s_en_rhs, g.count())
                    pool.wait_ge(s_inv, g.count())
                    if g.has(1):
                        pool.wait_ge(s_G, g.count(1))
                    nc.gpsimd.tensor_tensor(beT[:, 0:N], inc[:, g.slot(2), 1, :],
                                            inv[:, g.plus(-1).slot(4), 1:2].broadcast_to([P, N]), ALU.mult).then_inc(s_beT, 1)
                    nc.gpsimd.tensor_copy(beT[:, N:N + 1], adj_in[:, g.slot(4), 1, 0:1]).then_inc(s_row, 1)
                g = t.plus(1)
                if g.within(NG):
                    s = g.slot(2)
                    if g.has(2):
                        pool.wait_ge(s_y_sb, g.count(2))
                    pool.wait_ge(s_h, g.count())
                    pool.wait_ge(s_x1, g.count())
                    nc.gpsimd.tensor_tensor(rest[:, s, :], x1[:, s, :], h[:, s, :], ALU.add).then_inc(s_xh, 1)
                    if g.base == 0:
                        pool.wait_ge(s_small, SMALL * 16)
                    pool.wait_ge(s_xh, g.count())
                    nc.gpsimd.tensor_tensor(rest[:, s, :], rest[:, s, :], b2_bc[:, :], ALU.add).then_inc(s_rest, 1)
                g = t
                if g.within(NG):
                    pool.wait_ge(s_G_hi, g.count())
                    if g.has(1):
                        pool.wait_ge(s_y, g.count(1))
                    nc.gpsimd.tensor_tensor(G_lo[:, :], G[:, g.slot(4), 0:N], G_hi[:, :],
                                            ALU.subtract).then_inc(s_G_lo, 1)
                    pool.wait_ge(s_z_hi, g.count())
                    if g.has(1):
                        pool.wait_ge(s_y, g.count(1))
                    nc.gpsimd.tensor_tensor(z_lo[:, :], z[:, :], z_hi[:, :], ALU.subtract).then_inc(s_z_lo, 1)

            turns(pool, turn, NG, {-2: setup_w0, 0: setup_w2})

        @block.scalar
        def _(act):
            act.wait_ge(k_ones, 18)
            nc.scalar.activation(en_rhs[0:32, :, :], head_rows[0:32, :].unsqueeze(2).broadcast_to([32, HEADS, N]), ACT.Copy).then_inc(k_rows, 1)
            nc.scalar.activation(es_lhs[32:64, :], ones[32:64, :], ACT.Copy).then_inc(k_rows, 1)

            def rounded(n):
                act.wait_ge(s_raw[n], 16)
                if n >= 3:
                    act.wait_ge(k_cent, n - 2)
                nc.scalar.activation(PIECES[n][1], piece(n), ACT.Copy).then_inc(k_hi, 1)

            def copy_sums():
                act.wait_ge(k_sums, 1)
                nc.scalar.activation(sums_sb[0:2, :], p_w1a[0:2, :], ACT.Copy).then_inc(k_sums_sb, 1)

            def copy_means():
                act.wait_ge(k_mean, 2)
                act.wait_ge(k_lo1, 2)
                nc.scalar.activation(mean_sb, p_w1a[:, :], ACT.Copy, scale=1.0 / DH).then_inc(k_mean_sb, 1)
                nc.scalar.activation(t_bc[:, :], p_tb[:, :], ACT.Copy).then_inc(k_mean_sb, 1)

            rounded(0)

            def exps(g, half):
                act.wait_ge(s_max, g.count(per=2) - 1 + half)
                for i in range(half * HH, (half + 1) * HH):
                    last = nc.scalar.activation(att[:, i, :], att[:, i, :], ACT.Exp, bias=neg_max[:, i:i + 1])
                last.then_inc(s_exp, 1)

            def turn(t):
                g = t.plus(2)
                if g.within(NG):
                    act.wait_ge(s_xnT, g.count())
                    if g.has(1):
                        act.wait_ge(s_feats, g.count(1))
                    nc.scalar.activation(h0[:, :, 0, :], p_ta[:, :].rearrange("p (c n) -> p c n", n=N), ACT.Relu).then_inc(s_h0_hi, 1)
                g = t.plus(1)
                if g.within(NG):
                    exps(g, 0)
                g = t
                if g.within(NG):
                    act.wait_ge(s_pre, g.count(per=2) - 1)
                    nc.scalar.activation(r[:, 0:HALF], r[:, 0:HALF], ACT.Relu).then_inc(s_r, 1)
                if t.plus(1).within(NG):
                    exps(t.plus(1), 1)
                if g.within(NG):
                    act.wait_ge(s_rT, g.count(per=2) - 1)
                    if g.has(1):
                        act.wait_ge(s_w2, g.count(1))
                    nc.scalar.activation(rT_hi[:, 0:HALF], p_ta[:, :], ACT.Copy).then_inc(s_rT_hi, 1)
                g = t.plus(1)
                if g.within(NG):
                    act.wait_ge(s_attT, g.count())
                    if g.has(1):
                        act.wait_ge(s_o, g.count(1))
                    nc.scalar.activation(attT[:, :, :].rearrange("p h n -> p (h n)"), p_att[:, :],
                                         ACT.Copy).then_inc(s_attT_sb, 1)
                g = t
                if g.within(NG):
                    act.wait_ge(s_pre, g.count(per=2))
                    nc.scalar.activation(r[:, HALF:DH], r[:, HALF:DH], ACT.Relu).then_inc(s_r, 1)
                if t.base == -1:
                    copy_sums()
                g = t.plus(2)
                if g.within(NG):
                    act.wait_ge(s_e, g.count())
                    if g.has(1):
                        act.wait_ge(s_e_rest, g.count(1))
                    nc.scalar.activation(e_hi[:, :], p_e[0:64, 0:N], ACT.Copy).then_inc(s_e_hi, 1)
                g = t.plus(3)
                if g.within(NG):
                    act.wait_ge(s_nb0, g.count())
                    if g.has(1):
                        act.wait_ge(s_xnT, g.count(1))
                    nc.scalar.activation(xn[:, :], x_in[:, g.slot(4), :], ACT.Identity, bias=nb0[:, :],
                                         scale=rs0[:, :]).then_inc(s_xn, 1)
                if t.base == -1:
                    copy_means()
                g = t
                if g.within(NG):
                    if g.has(1):
                        act.wait_ge(s_y, g.count(1))
                    nc.scalar.activation(G_hi[:, :], G[:, g.slot(4), 0:N], ACT.Copy).then_inc(s_G_hi, 1)
                g = t
                if g.within(NG):
                    act.wait_ge(s_rT, g.count(per=2))
                    nc.scalar.activation(rT_hi[:, HALF:DH], p_tb[:, :], ACT.Copy).then_inc(s_rT_hi, 1)
                g = t.plus(1)
                if g.within(NG):
                    act.wait_ge(s_nb1, g.count())
                    if g.has(2):
                        act.wait_ge(s_hg, g.count(2))
                        act.wait_ge(s_xh, g.count(2))
                    nc.scalar.activation(h[:, g.slot(2), :], x1[:, g.slot(2), :], ACT.Relu, bias=nb1[:, :],
                                         scale=rs1[:, :]).then_inc(s_h, 1)
                    if g.base == 0:
                        rounded(3)
                    act.wait_ge(s_hg, g.count())
                    if g.has(1):
                        act.wait_ge(s_w1, g.count(1, per=2))
                    nc.scalar.activation(hg_hi[:, :], p_w1b[:, :], ACT.Copy).then_inc(s_hg_hi, 1)
                g = t.plus(2)
                if g.within(NG):
                    for b in range(2):
                        act.wait_ge(s_scores, g.count(per=2) - 1 + b)
                        if b == 0 and g.has(1):
                            act.wait_ge(s_attT, g.count(1))
                        nc.scalar.activation(att[:, b * HH:(b + 1) * HH, :].rearrange("p h n -> p (h n)"),
                                             p_att[:, b * HALF:(b + 1) * HALF], ACT.Copy, scale=SLOPE).then_inc(s_sloped, 1)
                    act.wait_ge(s_G, g.count())
                    if g.has(4):
                        act.wait_ge(s_y, g.count(4))
                    nc.scalar.activation(G[:, g.slot(4), 0:N + 1], p_G, ACT.Copy).then_inc(s_G_sb, 1)
                g = t
                if g.within(NG):
                    act.wait_ge(s_z, g.count())
                    if g.has(1):
                        act.wait_ge(s_y, g.count(1))
                    nc.scalar.activation(z_hi[:, :], z[:, :], ACT.Copy).then_inc(s_z_hi, 1)

            def setup_w1a():
                rounded(1)

            def setup_w1b():
                rounded(2)

            def setup_w2b():
                rounded(4)

            turns(act, turn, NG, {-2: setup_w1a, -1: setup_w1b, 0: setup_w2b})

        @block.vector
        def _(dve):
            nc.vector.memset(Wa[:, :, :].bitcast(F32), 0.0).then_inc(k_wa0, 1)

            def setup_wa():
                dve.wait_ge(s_raw[0], 16)
                dve.wait_ge(s_vectors, 32)
                for c in range(DC):
                    if c >= 2:
                        dve.wait_ge(k_pulled, c - 1)
                    nc.vector.tensor_tensor(prod_self[:, c % 2 * D:(c % 2 + 1) * D], piece(0)[:, c, :], a_bc[:, 0, :],
                                            ALU.mult).then_inc(k_prod_self, 1)
                    dve.wait_ge(k_prod_self, c + 1)
                    nc.vector.reduce_sum(wa_raw[:, 0, c, :], prod_self[:, c % 2 * D:(c % 2 + 1) * D].rearrange("p (h u) -> p h u", u=UN),
                                         X).then_inc(k_pulled, 1)
                for c in range(DC):
                    dve.wait_ge(k_prod_neigh, c + 1)
                    nc.vector.reduce_sum(wa_raw[:, 1, c, :], prod_neigh[c].rearrange("p (h u) -> p h u", u=UN),
                                         X).then_inc(k_pulled, 1)
                dve.wait_ge(k_pulled, 2 * DC)
                dve.wait_ge(k_wa0, 1)
                for a in range(2):
                    first = 32 * a
                    for i in range(2):
                        nc.vector.tensor_copy(Wa[:, :, first + i * HEADS:first + (i + 1) * HEADS], wa_raw[:, a, :, :]).then_inc(k_wa, 1)
                    dve.wait_ge(k_wa, 3 * a + 2)
                    nc.vector.tensor_tensor(Wa[:, :, first + 2 * HEADS:first + 3 * HEADS], wa_raw[:, a, :, :],
                                            Wa[:, :, first:first + HEADS], ALU.subtract).then_inc(k_wa, 1)
                dve.wait_ge(k_ones, 18)
                nc.vector.reduce_sum(lo_rows[:, :], lo_rows8[:, :], X).then_inc(k_lorow, 1)
                dve.wait_ge(k_lorow, 1)

            def rest_of(n):
                dve.wait_ge(k_hi, n + 1)
                nc.vector.tensor_tensor(PIECES[n][2], piece(n), PIECES[n][1], ALU.subtract).then_inc(k_lo1, 1)

            def centre(m):
                for c in range(CB):
                    last = nc.vector.scalar_tensor_tensor(
                        piece(3 + m)[:, c, :], piece(3 + m)[:, c, :], gamma_beta[:, 0, m * CB + c:m * CB + c + 1],
                        mean_sb, ALU.mult, ALU.subtract)
                last.then_inc(k_cent, 1)

            def turn(t):
                g = t.plus(1)
                if g.within(NG):
                    for b in range(2):
                        half = att[:, b * HH:(b + 1) * HH, :].rearrange("p h n -> p (h n)")
                        dve.wait_ge(s_sloped, g.count(per=2) - 1 + b)
                        nc.vector.tensor_tensor(half, p_att[:, b * HALF:(b + 1) * HALF], half, ALU.max).then_inc(s_leaky, 1)
                    for b in range(2):
                        half = att[:, b * HH:(b + 1) * HH, :]
                        dve.wait_ge(s_leaky, g.count(per=2) - 1 + b)
                        if b == 0:
                            dve.wait_ge(s_mask, g.count())
                        nc.vector.tensor_tensor(half, half, mask[:, :].unsqueeze(1).broadcast_to([P, HH, N]),
                                                ALU.add).then_inc(s_masked, 1)
                    for b in range(2):
                        dve.wait_ge(s_masked, g.count(per=2) - 1 + b)
                        nc.vector.reduce_max(neg_max[:, b * HH:(b + 1) * HH], att[:, b * HH:(b + 1) * HH, :], X,
                                             negate=True).then_inc(s_max, 1)
                g = t
                if g.within(NG):
                    dve.wait_ge(s_w1, g.count(per=2) - 1)
                    dve.wait_ge(s_inv, g.plus(1).count())
                    if g.has(1):
                        dve.wait_ge(s_rT, g.count(1, per=2))
                    nc.vector.scalar_tensor_tensor(r[:, 0:HALF], p_w1a[:, :], inv[:, g.slot(4), 0:1],
                                                   b1_bc[:, 0:HALF], ALU.mult, ALU.add).then_inc(s_pre, 1)
                g = t.plus(2)
                if g.within(NG):
                    dve.wait_ge(s_h0_hi, g.count())
                    nc.vector.scalar_tensor_tensor(h0[:, :, 1, :], p_ta[:, :].rearrange("p (c n) -> p c n", n=N), 0.0, h0[:, :, 0, :],
                                                   ALU.max, ALU.subtract).then_inc(s_h0_lo, 1)
                    dve.wait_ge(s_in[g.slot(4)], g.uses(4, 32))
                    if g.has(2):
                        dve.wait_ge(s_G, g.count(2))
                        dve.wait_ge(s_beT, g.count(2))
                    nc.vector.tensor_scalar(inc[:, g.slot(2), :, :], adj_in[:, g.slot(4), :, :], 0.0, None,
                                            ALU.not_equal).then_inc(s_inc, 1)
                    dve.wait_ge(s_inc, g.count())
                    nc.vector.reduce_sum(G[:, g.plus(-1).slot(4), N + 1:N + 2], inc[:, g.slot(2), 1, :], X).then_inc(s_sizes, 1)
                g = t.plus(-1)
                if g.within(NG):
                    dve.wait_ge(s_y, g.count())
                    dve.wait_ge(s_rest, g.count())
                    if g.has(2):
                        dve.wait_ge(s_out[g.slot(2)], g.plus(-2).uses(2, 16))
                    nc.vector.scalar_tensor_tensor(y[:, g.slot(2), :], p_tb[:, :], inv[:, g.slot(4), 0:1],
                                                   rest[:, g.slot(2), :], ALU.mult, ALU.add).then_inc(s_y_sb, 1)
                g = t.plus(1)
                if g.within(NG):
                    dve.wait_ge(s_feats, g.count())
                    if g.base == 0:
                        dve.wait_ge(s_small, SMALL * 16)
                    if g.has(2):
                        dve.wait_ge(s_o, g.count(2))
                    nc.vector.tensor_tensor(feats[:, g.slot(2), :, 0:UN],
                                            p_f[:, :].rearrange("p (h u) -> p h u", u=UN),
                                            b0_bc[:, :].rearrange("p (h u) -> p h u", u=UN),
                                            ALU.add).then_inc(s_feats_sb, 1)
                g = t
                if g.within(NG):
                    dve.wait_ge(s_r, g.count(per=2) - 1)
                    nc.vector.bn_stats(st2[:, 0, :], r[:, 0:HALF]).then_inc(s_stats2, 1)
                g = t.plus(3)
                if g.within(NG):
                    dve.wait_ge(s_in[g.slot(4)], g.uses(4, 32))
                    nc.vector.bn_stats(st0[:, :], x_in[:, g.slot(4), :]).then_inc(s_stats0, 1)
                    dve.wait_ge(s_stats0, g.count())
                g = t
                if g.within(NG):
                    dve.wait_ge(s_w1, g.count(per=2))
                    nc.vector.scalar_tensor_tensor(r[:, HALF:DH], p_w1b[:, :], inv[:, g.slot(4), 0:1],
                                                   b1_bc[:, HALF:DH], ALU.mult, ALU.add).then_inc(s_pre, 1)
                g = t.plus(3)
                if g.within(NG):
                    nc.vector.bn_aggr(mv0[:, :], st0[:, :]).then_inc(s_mv0, 1)
                g = t
                if g.within(NG):
                    dve.wait_ge(s_rT_hi, g.count(per=2) - 1)
                    nc.vector.tensor_tensor(rT_lo[:, 0:HALF], p_ta[:, :], rT_hi[:, 0:HALF],
                                            ALU.subtract).then_inc(s_rT_lo, 1)
                    dve.wait_ge(s_r, g.count(per=2))
                    nc.vector.bn_stats(st2[:, 1, :], r[:, HALF:DH]).then_inc(s_stats2, 1)
                    dve.wait_ge(s_stats2, g.count(per=2))
                if t.base == -1:
                    rest_of(2)
                g = t.plus(2)
                if g.within(NG):
                    dve.wait_ge(s_e_hi, g.count())
                    nc.vector.tensor_tensor(e_rest[:, :], p_e[0:64, N:2 * N], e_hi[:, :], ALU.subtract).then_inc(s_e_rest, 1)
                if t.within(NG):
                    nc.vector.bn_aggr(mv2[:, :], st2[:, :, :].rearrange("p a b -> p (a b)")).then_inc(s_mv2, 1)
                if g.within(NG):
                    dve.wait_ge(s_e_rest, g.count())
                    if g.has(1):
                        dve.wait_ge(s_en_rhs, g.count(1))
                    nc.vector.scalar_tensor_tensor(en_parts[32:64, :], e_rest[32:64, :], lo_rows[32:64, :], p_e[32:64, 0:N],
                                                   ALU.mult, ALU.add).then_inc(s_en_parts, 1)
                    if g.has(1):
                        dve.wait_ge(s_scores, g.count(1, per=2))
                    nc.vector.scalar_tensor_tensor(es_lhs[0:32, :], e_rest[0:32, :], lo_rows[0:32, :], p_e[0:32, 0:N],
                                                   ALU.mult, ALU.add).then_inc(s_es_lhs, 1)
                if t.base == -2:
                    rest_of(1)
                g = t.plus(1)
                if g.within(NG):
                    s = g.slot(2)
                    dve.wait_ge(s_o, g.count())
                    nc.vector.reciprocal(rden[:, :].rearrange("p (b h) -> p b h", b=2), p_o[:, :, :, UN]).then_inc(s_rden, 1)
                g = t.plus(2)
                if g.within(NG + 1):
                    if g.within(NG):
                        dve.wait_ge(s_sizes, g.count())
                    if g.has(1):
                        dve.wait_ge(s_G_sb, g.count(1))
                    nc.vector.tensor_scalar(cnt[:, :], G[:, g.plus(-1).slot(4), N:N + 2], TINY, None, ALU.max).then_inc(s_cnt1, 1)
                g = t.plus(1)
                if g.within(NG):
                    dve.wait_ge(s_rden, g.count())
                    nc.vector.tensor_tensor(o_sc[:, :].rearrange("p (b h u) -> p b h u", b=2, u=UN),
                                            p_o[:, :, :, 0:UN],
                                            rden[:, :].rearrange("p (b h) -> p b h", b=2).unsqueeze(3).broadcast_to([P, 2, HH, UN]),
                                            ALU.mult).then_inc(s_osc, 1)
                if t.plus(2).within(NG + 1):
                    dve.wait_ge(s_cnt1, t.plus(2).count())
                    nc.vector.reciprocal(inv0[:, :], cnt[:, :]).then_inc(s_inv0, 1)
                if t.within(NG):
                    dve.wait_ge(s_rT_hi, t.count(per=2))
                    nc.vector.tensor_tensor(rT_lo[:, HALF:DH], p_tb[:, :], rT_hi[:, HALF:DH],
                                            ALU.subtract).then_inc(s_rT_lo, 1)
                if g.within(NG):
                    dve.wait_ge(s_osc, g.count())
                    if g.has(2):
                        dve.wait_ge(s_xh, g.count(2))
                    nc.vector.scalar_tensor_tensor(x1[:, s, :], o_sc[:, :], 0.0, x_in[:, g.slot(4), :],
                                                   ALU.max, ALU.add).then_inc(s_x1, 1)
                    dve.wait_ge(s_x1, g.count())
                    nc.vector.bn_stats(st1[:, :], x1[:, s, :]).then_inc(s_stats1, 1)
                    dve.wait_ge(s_stats1, g.count())
                g = t.plus(2)
                if g.within(NG + 1):
                    dve.wait_ge(s_inv0, g.count())
                    if g.has(4):
                        dve.wait_ge(s_beT, g.count(4))
                    nc.vector.scalar_tensor_tensor(inv[:, g.plus(-1).slot(4), :], G[:, g.plus(-1).slot(4), N:N + 2], 0.0, inv0[:, :],
                                                   ALU.is_gt, ALU.mult).then_inc(s_inv, 1)
                g = t.plus(1)
                if g.within(NG):
                    nc.vector.bn_aggr(mv1[:, :], st1[:, :]).then_inc(s_mv1, 1)
                if t.base == -1:
                    dve.wait_ge(k_mean_sb, 2)
                    centre(0)
                    centre(1)
                g = t
                if g.within(NG):
                    dve.wait_ge(s_w2, g.count())
                    dve.wait_ge(s_rs2, g.count())
                    if g.has(1):
                        dve.wait_ge(s_z_lo, g.count(1))
                    nc.vector.scalar_tensor_tensor(z[:, :], p_w1a[:, :], rs2[:, :], t_bc[:, :],
                                                   ALU.mult, ALU.add).then_inc(s_z, 1)
                g = t.plus(1)
                if g.within(NG):
                    dve.wait_ge(s_hg_hi, g.count())
                    nc.vector.tensor_tensor(hg_lo[:, :], p_w1b[:, :], hg_hi[:, :], ALU.subtract).then_inc(s_hg_lo, 1)

            turns(dve, turn, NG, {-2: setup_wa})

        @block.tensor
        def _(pe):
            mm = nc.tensor.matmul
            pe.wait_ge(k_ident, 1)

            def setup_e():
                pe.wait_ge(k_wa, 6)
                pe.wait_ge(k_rows, 2)

            def sums():
                pe.wait_ge(s_raw[3], 16)
                pe.wait_ge(s_raw[4], 16)
                pe.wait_ge(s_small, SMALL * 16)
                for c in range(HC):
                    last = mm(p_w1a[0:2, :], gamma_beta[:, :, c],
                              piece(3 + c // CB)[:, c % CB, :], start=c == 0, stop=c == HC - 1)
                last.then_inc(k_sums, 1)

            def spread():
                pe.wait_ge(k_sums_sb, 1)
                for row, dst in ((0, p_w1a), (1, p_tb)):
                    mm(dst[:, :], ident[0:2, row:row + 1].broadcast_to([2, P]), sums_sb[0:2, :],
                       start=True, stop=True).then_inc(k_mean, 1)

            def three(dst, hi, lo, w_hi, w_lo, first, final):
                mm(dst, hi, w_hi, start=first, stop=False)
                mm(dst, hi, w_lo, start=False, stop=False)
                return mm(dst, lo, w_hi, start=False, stop=final)

            def hidden(g, half, dst):
                for c in range(DC):
                    k = slice(c * P, (c + 1) * P)
                    n = slice(half * HALF, (half + 1) * HALF)
                    last = three(dst[:, :], hg_hi[:, k], hg_lo[:, k], W1_hi[:, c, n], W1_lo[:, c, n], c == 0, c == DC - 1)
                last.then_inc(s_w1, 1)

            def features(c):
                return three(p_f[:, :], h0[:, c, 0, :], h0[:, c, 1, :], W0_hi[:, c, :], W0_lo[:, c, :], c == 0, c == DC - 1)

            def transposes(dst, src, s):
                for c in range(HALF // P):
                    last = nc.tensor.transpose(dst[:, c * P:(c + 1) * P], src[:, c * P:(c + 1) * P], ident[:, :])
                last.then_inc(s, 1)

            def turn(t):
                g = t
                if g.within(NG):
                    pe.wait_ge(s_hg_lo, g.count())
                    if g.has(1):
                        pe.wait_ge(s_z, g.count(1))
                    hidden(g, 0, p_w1a)
                g = t.plus(-1)
                if g.within(NG):
                    pe.wait_ge(s_z_lo, g.count())
                    pe.wait_ge(s_G_lo, g.count())
                    pe.wait_ge(s_rT_lo, g.count(per=2))
                    three(p_tb[:, :], G_hi[:, :], G_lo[:, :], z_hi[:, :], z_lo[:, :],
                          True, True).then_inc(s_y, 1)
                g = t
                if g.within(NG):
                    hidden(g, 1, p_w1b)
                g = t
                if g.within(NG):
                    pe.wait_ge(s_r, g.count(per=2) - 1)
                    if g.plus(2).within(NG):
                        pe.wait_ge(s_h0_lo, g.plus(2).count())
                    transposes(p_ta, r[:, 0:HALF], s_rT)
                g = t.plus(1)
                if g.within(NG):
                    pe.wait_ge(s_exp, g.count(per=2))
                    for i in range(HEADS):
                        last = nc.tensor.transpose(p_att[:, i * N:(i + 1) * N], att[:, i, :], ident[:, :])
                    last.then_inc(s_attT, 1)
                g = t.plus(2)
                if g.within(NG):
                    pe.wait_ge(s_h0_lo, g.count())
                    if g.has(1):
                        pe.wait_ge(s_es_lhs, g.count(1))
                        pe.wait_ge(s_G_sb, g.count(1))
                    for c in range(DC):
                        last = mm(p_e, Wa[:, c, :], h0[:, c, :, :].rearrange("p a n -> p (a n)"), start=c == 0, stop=c == DC - 1)
                    last.then_inc(s_e, 1)
                g = t.plus(2)
                if g.within(NG):
                    if g.base == 0:
                        pe.wait_ge(k_lo0, 1)
                    if g.has(1):
                        pe.wait_ge(s_feats_sb, g.count(1))
                    for c in range(DC - 2):
                        features(c)
                g = t.plus(1)
                if g.within(NG):
                    pe.wait_ge(s_attT_sb, g.count())
                    pe.wait_ge(s_feats_sb, g.count())
                    for i in range(HEADS):
                        last = mm(p_o[:, i // HH, i % HH, :], attT[:, i, :], feats[:, g.slot(2), i, :], start=True, stop=True)
                    last.then_inc(s_o, 1)
                if t.base == -1:
                    spread()
                g = t
                if g.within(NG):
                    pe.wait_ge(s_r, g.count(per=2))
                    if g.has(1):
                        pe.wait_ge(s_y_sb, g.count(1))
                    transposes(p_tb, r[:, HALF:DH], s_rT)
                g = t
                if g.within(NG):
                    for c in range(HC):
                        if c % CB == 0:
                            if g.base == 0:
                                pe.wait_ge(k_lo2, 1 + c // CB)
                            pe.wait_ge(s_rT_lo, g.count(per=2) - 1 + c // CB)
                        k = slice(c * P, (c + 1) * P)
                        last = three(p_w1a[:, :], rT_hi[:, k], rT_lo[:, k], W2_hi[:, c, :], W2_lo[:, c, :], c == 0, c == HC - 1)
                    last.then_inc(s_w2, 1)
                if t.plus(2).within(NG):
                    features(DC - 2)
                g = t.plus(1)
                if g.within(NG):
                    pe.wait_ge(s_h, g.count())
                    pe.wait_ge(s_G_sb, g.count())
                    if g.has(1):
                        pe.wait_ge(s_pre, g.count(1, per=2))
                    for c in range(DC):
                        last = mm(p_w1b[:, c * P:(c + 1) * P], h[:, g.slot(2), c * P:(c + 1) * P], G[:, g.slot(4), 0:N],
                                  start=True, stop=True)
                    last.then_inc(s_hg, 1)
                g = t.plus(2)
                if g.within(NG):
                    features(DC - 1).then_inc(s_feats, 1)
                    pe.wait_ge(s_en_rhs, g.count())
                    pe.wait_ge(s_es_lhs, g.count())
                    if g.has(1):
                        pe.wait_ge(s_osc, g.count(1))
                    for b in range(2):
                        dst = p_att[:, b * HALF:(b + 1) * HALF]
                        last = mm(dst, es_lhs[:, :], en_rhs[:, b * HH:(b + 1) * HH, :].rearrange("p h n -> p (h n)"),
                                  start=True, stop=True)
                        last.then_inc(s_scores, 1)
                    pe.wait_ge(s_beT, g.count())
                    pe.wait_ge(s_row, g.count())
                    if g.has(1):
                        pe.wait_ge(s_G_sb, g.count(1))
                    mm(p_G, inc[:, g.slot(2), 1, :], beT[:, :], start=True, stop=True).then_inc(s_G, 1)
                g = t.plus(3)
                if g.within(NG):
                    pe.wait_ge(s_xn, g.count())
                    if t.within(NG):
                        pe.wait_ge(s_rT_lo, t.count(per=2) - 1)
                    elif g.has(1):
                        pe.wait_ge(s_h0_lo, g.count(1))
                    transposes(p_ta, xn, s_xnT)

            def setup_w1():
                pe.wait_ge(k_lo1, 2)
                pe.wait_ge(k_mean_sb, 2)

            turns(pe, turn, NG, {-2: setup_e, -1: sums, 0: setup_w1})


_INS = ["x", "adj2", "W0T", "b0", "a_self", "a_neigh", "W1T", "b1", "gammaT", "betaT", "W2T", "b2"]


def kernel(x, adj, L0_gnn_W, L0_gnn_b, L0_gnn_a_self, L0_gnn_a_neigh, L1_gnn_W1, L1_gnn_b1, L1_gnn_gamma,
           L1_gnn_beta, L1_gnn_W2, L1_gnn_b2):
    import numpy as np
    import concourse.bacc as bacc
    from concourse.bass_utils import run_bass_kernel_spmd

    adj = np.asarray(adj)
    f = np.asarray(L0_gnn_W).shape[1]
    laid = {
        "x": x,
        "adj2": np.stack([adj, adj.transpose(0, 2, 1)], axis=2),
        "W0T": np.asarray(L0_gnn_W).transpose(1, 0, 2).reshape(f, -1),
        "b0": L0_gnn_b, "a_self": L0_gnn_a_self, "a_neigh": L0_gnn_a_neigh,
        "W1T": np.asarray(L1_gnn_W1).T, "b1": L1_gnn_b1,
        "gammaT": np.asarray(L1_gnn_gamma).reshape(-1, P).T, "betaT": np.asarray(L1_gnn_beta).reshape(-1, P).T,
        "W2T": np.asarray(L1_gnn_W2).T, "b2": L1_gnn_b2,
    }
    nc = bacc.Bacc("TRN2", target_bir_lowering=False, num_devices=1)
    arrays, args = {}, []
    for name in _INS:
        a = np.ascontiguousarray(laid[name])
        arrays[f"in_{name}"] = a
        args.append(nc.dram_tensor(f"in_{name}", a.shape, mybir.dt.from_np(a.dtype), kind="ExternalInput").ap())
    out = nc.dram_tensor("out", arrays["in_x"].shape, F32, kind="ExternalOutput").ap()
    gnn_two_layers(nc, *args, out)
    got = run_bass_kernel_spmd(nc, [arrays], core_ids=[0])
    return got.results[0]["out"]
```
